# Optimizing a Trainium2 kernel written in Bass

```python
import numpy as np
import jax
import jax.numpy as jnp

def _softmax(x, axis=-1):
    return jax.nn.softmax(x, axis=axis)

def _gelu(x):
    return jax.nn.gelu(x, approximate=True)

def _silu(x):
    return jax.nn.silu(x)

def _sigmoid(x):
    return jax.nn.sigmoid(x)

def _layernorm(x, axis=-1, eps=1e-05):
    m = jnp.mean(x, axis=axis, keepdims=True)
    v = jnp.var(x, axis=axis, keepdims=True)
    return (x - m) / jnp.sqrt(v + eps)

def _scatter_add(tgt, idx, src, axis=0):
    return tgt.at[idx].add(src)

def _segment_sum(src, seg, n):
    return jax.ops.segment_sum(src, seg, n)
kernel_name = 'mk_adj_preln_d4_adj_r2_f5057c'

def setup_inputs(seed: int=0):
    np.random.seed(seed)
    _w = jnp.asarray

    def _rec_inputs():
        import jax
        import jax.numpy as jnp
        _gk = jax.random.key(seed)
        x = -0.0005207 + 1.001 * jax.random.normal(jax.random.fold_in(_gk, 1), (4096, 128), jnp.float32)
        _w = (1.0 + jnp.arange(4096, dtype=jnp.float32)) ** (-0.5)
        _w = _w / _w.mean()
        _pij = jnp.clip(0.000976562 * _w[:, None] * _w[None, :], 0.0, 1.0)
        _a = jax.random.uniform(jax.random.fold_in(_gk, 2), (4096, 4096)) < _pij
        _a = jnp.logical_or(_a, jnp.eye(4096, dtype=bool))
        _af = _a.astype(jnp.float32)
        _af = _af * jax.random.uniform(jax.random.fold_in(_gk, 3), (4096, 4096), jnp.float32, 0.05, 1)
        adj = _af
        return (x, adj)
    x, adj = _rec_inputs()

    def _L0_gnn_setup():
        import jax, jax.numpy as jnp
        import numpy as np
        IN_DIM = 128
        OUT_DIM = 128
        N = 8192
        key = jax.random.key(seed)
        k_x, k_adj, k_w, k_b = jax.random.split(key, 4)
        x = jax.random.normal(k_x, (N, IN_DIM), dtype=jnp.float32)
        adj = jax.random.uniform(k_adj, (N, N), dtype=jnp.float32)
        bound = 1.0 / np.sqrt(2 * IN_DIM)
        W = jax.random.uniform(k_w, (OUT_DIM, 2 * IN_DIM), dtype=jnp.float32, minval=-bound, maxval=bound)
        b = jax.random.uniform(k_b, (OUT_DIM,), dtype=jnp.float32, minval=-bound, maxval=bound)
        return {'x': x, 'adj': adj, 'W': W, 'b': b}
    _L0_gnn_all = _L0_gnn_setup()
    _L0_gnn_in = {k: v for k, v in _L0_gnn_all.items() if k in ('W', 'b')}
    del _L0_gnn_all

    def _L1_gnn_setup():
        import jax, jax.numpy as jnp
        import numpy as np
        EPS = 1e-12
        key = jax.random.key(seed)
        k1, k2, k3, k4 = jax.random.split(key, 4)
        N, F_IN, F_OUT = (4096, 128, 128)
        x = jax.random.normal(k1, (N, F_IN), dtype=jnp.float32)
        adj = jax.random.uniform(k2, (N, N), dtype=jnp.float32)
        gain = float(np.sqrt(2.0))
        limit = gain * float(np.sqrt(6.0 / (F_IN + F_OUT)))
        W = jax.random.uniform(k3, (F_OUT, F_IN), dtype=jnp.float32, minval=-limit, maxval=limit)
        b = jax.random.uniform(k4, (F_OUT,), dtype=jnp.float32, minval=-1.0 / np.sqrt(F_IN), maxval=1.0 / np.sqrt(F_IN))
        return {'x': x, 'adj': adj, 'W': W, 'b': b}
    _L1_gnn_all = _L1_gnn_setup()
    _L1_gnn_in = {k: v for k, v in _L1_gnn_all.items() if k in ('W', 'b')}
    del _L1_gnn_all

    def _L2_gnn_setup():
        import jax, jax.numpy as jnp
        import numpy as np
        N, DIM = (8192, 128)

        def _gru_cell(x, h, W_ih, W_hh, b_ih, b_hh):
            gi = x @ W_ih.T + b_ih
            gh = h @ W_hh.T + b_hh
            i_r, i_z, i_n = jnp.split(gi, 3, axis=-1)
            h_r, h_z, h_n = jnp.split(gh, 3, axis=-1)
            r = jax.nn.sigmoid(i_r + h_r)
            z = jax.nn.sigmoid(i_z + h_z)
            n = jnp.tanh(i_n + r * h_n)
            return (1.0 - z) * n + z * h
        key = jax.random.key(seed)
        ks = jax.random.split(key, 8)
        states = jax.random.normal(ks[0], (N, DIM), dtype=jnp.float32)
        adj = jax.random.uniform(ks[1], (N, N), dtype=jnp.float32)
        s = 1.0 / np.sqrt(DIM)
        W_msg = jax.random.uniform(ks[2], (DIM, DIM), minval=-s, maxval=s, dtype=jnp.float32)
        b_msg = jax.random.uniform(ks[3], (DIM,), minval=-s, maxval=s, dtype=jnp.float32)
        W_ih = jax.random.uniform(ks[4], (3 * DIM, DIM), minval=-s, maxval=s, dtype=jnp.float32)
        W_hh = jax.random.uniform(ks[5], (3 * DIM, DIM), minval=-s, maxval=s, dtype=jnp.float32)
        b_ih = jax.random.uniform(ks[6], (3 * DIM,), minval=-s, maxval=s, dtype=jnp.float32)
        b_hh = jax.random.uniform(ks[7], (3 * DIM,), minval=-s, maxval=s, dtype=jnp.float32)
        return {'states': states, 'adj': adj, 'W_msg': W_msg, 'b_msg': b_msg, 'W_ih': W_ih, 'W_hh': W_hh, 'b_ih': b_ih, 'b_hh': b_hh}
    _L2_gnn_all = _L2_gnn_setup()
    _L2_gnn_in = {k: v for k, v in _L2_gnn_all.items() if k in ('W_msg', 'b_msg', 'W_ih', 'W_hh', 'b_ih', 'b_hh')}
    del _L2_gnn_all

    def _L3_gnn_setup():
        import jax, jax.numpy as jnp
        import numpy as np

        def _lap_mul(A, x):
            d = 1.0 / jnp.sqrt(jnp.sum(A, axis=-1))
            return d[:, None] * (A @ (d[:, None] * x))
        key = jax.random.key(seed)
        k1, k2, k3, k4, k5, k6 = jax.random.split(key, 6)
        N, D_IN, D_OUT = (2048, 128, 128)
        x = jax.random.normal(k1, (N, D_IN), dtype=jnp.float32)
        A = jax.random.uniform(k2, (N, N), dtype=jnp.float32)
        s1 = 1.0 / np.sqrt(D_IN)
        W1 = jax.random.uniform(k3, (D_IN, D_OUT), minval=-s1, maxval=s1, dtype=jnp.float32)
        b1 = jax.random.uniform(k4, (D_OUT,), minval=-s1, maxval=s1, dtype=jnp.float32)
        W2 = jax.random.uniform(k5, (D_IN, D_OUT), minval=-s1, maxval=s1, dtype=jnp.float32)
        b2 = jax.random.uniform(k6, (D_OUT,), minval=-s1, maxval=s1, dtype=jnp.float32)
        return {'x': x, 'A': A, 'W1': W1, 'b1': b1, 'W2': W2, 'b2': b2, 'sigma': 1, 'k': 4}
    _L3_gnn_all = _L3_gnn_setup()
    _L3_gnn_in = {k: v for k, v in _L3_gnn_all.items() if k in ('W1', 'b1', 'W2', 'b2')}
    del _L3_gnn_all
    return {'x': x, 'adj': adj, 'L0_gnn_W': _L0_gnn_in['W'], 'L0_gnn_b': _L0_gnn_in['b'], 'L1_gnn_W': _L1_gnn_in['W'], 'L1_gnn_b': _L1_gnn_in['b'], 'L2_gnn_W_msg': _L2_gnn_in['W_msg'], 'L2_gnn_b_msg': _L2_gnn_in['b_msg'], 'L2_gnn_W_ih': _L2_gnn_in['W_ih'], 'L2_gnn_W_hh': _L2_gnn_in['W_hh'], 'L2_gnn_b_ih': _L2_gnn_in['b_ih'], 'L2_gnn_b_hh': _L2_gnn_in['b_hh'], 'L3_gnn_W1': _L3_gnn_in['W1'], 'L3_gnn_b1': _L3_gnn_in['b1'], 'L3_gnn_W2': _L3_gnn_in['W2'], 'L3_gnn_b2': _L3_gnn_in['b2']}

def reference(x, adj, L0_gnn_W, L0_gnn_b, L1_gnn_W, L1_gnn_b, L2_gnn_W_msg, L2_gnn_b_msg, L2_gnn_W_ih, L2_gnn_W_hh, L2_gnn_b_ih, L2_gnn_b_hh, L3_gnn_W1, L3_gnn_b1, L3_gnn_W2, L3_gnn_b2):
    import jax
    import jax.numpy as jnp

    def _L0_gnn_ref(x, adj, W, b):
        import jax, jax.numpy as jnp
        import numpy as np
        IN_DIM = 128
        OUT_DIM = 128
        N = 8192
        h_N = jnp.matmul(adj, x)
        h_cat = jnp.concatenate([x, h_N], axis=-1)
        out = jnp.maximum(jnp.einsum('nd,od->no', h_cat, W) + b, 0.0)
        return out

    def _L1_gnn_ref(x, adj, W, b):
        import jax, jax.numpy as jnp
        import numpy as np
        EPS = 1e-12
        N = adj.shape[0]
        a = adj + jnp.eye(N, dtype=adj.dtype)
        dinv = jax.lax.rsqrt(jnp.sum(a, axis=-1))
        a = a * dinv[:, None] * dinv[None, :]
        h = a @ x
        h = h @ W.T + b
        norm = jnp.linalg.norm(h, axis=1, keepdims=True)
        return h / jnp.maximum(norm, EPS)

    def _L2_gnn_ref(states, adj, W_msg, b_msg, W_ih, W_hh, b_ih, b_hh):
        import jax, jax.numpy as jnp
        import numpy as np
        N, DIM = (8192, 128)

        def _gru_cell(x, h, W_ih, W_hh, b_ih, b_hh):
            gi = x @ W_ih.T + b_ih
            gh = h @ W_hh.T + b_hh
            i_r, i_z, i_n = jnp.split(gi, 3, axis=-1)
            h_r, h_z, h_n = jnp.split(gh, 3, axis=-1)
            r = jax.nn.sigmoid(i_r + h_r)
            z = jax.nn.sigmoid(i_z + h_z)
            n = jnp.tanh(i_n + r * h_n)
            return (1.0 - z) * n + z * h
        agg = adj @ states
        msg = jax.nn.relu(agg @ W_msg.T + b_msg)
        return _gru_cell(msg, states, W_ih, W_hh, b_ih, b_hh)

    def _L3_gnn_ref(x, A, W1, b1, W2, b2, sigma, k):
        import jax, jax.numpy as jnp
        import numpy as np

        def _lap_mul(A, x):
            d = 1.0 / jnp.sqrt(jnp.sum(A, axis=-1))
            return d[:, None] * (A @ (d[:, None] * x))
        z = _lap_mul(A, x) @ W1 + b1
        z = jax.nn.leaky_relu(z, negative_slope=0.1)
        sq = jnp.sum(z * z, axis=-1)
        d2 = sq[:, None] + sq[None, :] - 2.0 * (z @ z.T)
        d2 = jnp.maximum(d2, 0.0)
        S = jnp.sqrt(d2 + 1e-10)
        S = jnp.exp(-S / (2.0 * sigma))
        order = jnp.argsort(-S, axis=-1)
        ranks = jnp.argsort(order, axis=-1)
        S = jnp.where(ranks < k, S, 0.0)
        A2 = S + A
        out = _lap_mul(A2, x) @ W2 + b2
        return out
    h = jnp.maximum(_layernorm(x, axis=-1), 0.0)
    x = x + _L0_gnn_ref(h, adj, L0_gnn_W, L0_gnn_b)
    h = jnp.maximum(_layernorm(x, axis=-1), 0.0)
    x = x + _L1_gnn_ref(h, adj, L1_gnn_W, L1_gnn_b)
    h = jnp.maximum(_layernorm(x, axis=-1), 0.0)
    x = x + _L2_gnn_ref(h, adj, L2_gnn_W_msg, L2_gnn_b_msg, L2_gnn_W_ih, L2_gnn_W_hh, L2_gnn_b_ih, L2_gnn_b_hh)
    h = jnp.maximum(_layernorm(x, axis=-1), 0.0)
    x = x + _L3_gnn_ref(h, adj, L3_gnn_W1, L3_gnn_b1, L3_gnn_W2, L3_gnn_b2, 1, 4)
    return x

_drawn_inputs = setup_inputs


def setup_inputs(seed=0):
    import zlib

    import numpy as np

    out = dict(_drawn_inputs(seed))
    spreads = {}
    factors = {'L1_gnn_b': 7.298,
     'L2_gnn_b_msg': 6.082,
     'L2_gnn_b_ih': 2.765,
     'L2_gnn_b_hh': 4.309,
     'L3_gnn_b1': 2.743}
    for name, (base, spread) in spreads.items():
        noise = np.random.default_rng([zlib.crc32(name.encode()), seed]).standard_normal(out[name].shape)
        drawn = base * np.exp(spread * noise) if base else spread * noise
        out[name] = jnp.asarray(drawn.astype(out[name].dtype))
    for name, factor in factors.items():
        out[name] = (out[name] * factor).astype(out[name].dtype)
    return out
```

```python
import concourse.bass as bass
from concourse import mybir
from contextlib import ExitStack

P = 128
N = 4096
BLK = 512
TPB = BLK // P
NB = N // BLK
NT = N // P
LAYERS = 5
SLOTS = 4
STREAMED = NB - 1
TOPK = 4
GSLOTS = 4

(IDENT, W_SELF, W_NEIGH, W_L1, W_MSG, W_IR, W_IZ, W_IN, W_HR, W_HZ, W_HN, W_LAP1, W_LAP2,
 ROW_L1, ROW_LAP1, ROW_LAP2) = range(16)
(C_L0, C_MSG, C_IR, C_IZ, C_IN, C_HR, C_HZ, C_HN) = range(8)
PACK = 16 * P + 8


class Steps:

    def __init__(self, eng, sem):
        self.eng, self.sem, self.base, self.n = eng, sem, 0, 0

    def add(self, ins):
        ins.then_inc(self.sem, 1)
        self.n += 1

    def value(self):
        return self.base + self.n

    def settle(self):
        self.eng.wait_ge(self.sem, self.value())

    def turn(self, base):
        self.base, self.n = base, 0


def streamed(m):
    return (m - 1) % SLOTS, (m - 1) // SLOTS


USES = [sum(1 for m in range(1, NB) if streamed(m)[0] == s) for s in range(SLOTS)]


def loaded_value(q, m):
    s, u = streamed(m)
    return 16 * (USES[s] * q + u + 1)


def previous_use(q, m):
    s, u = streamed(m)
    if u:
        return STREAMED * q + m - SLOTS
    return STREAMED * (q - 1) + 1 + s + SLOTS * (USES[s] - 1)


def gnn_stack(nc, x_in, at_in, pack_in, scaled_rows, out):
    fp32, bf16, u32 = mybir.dt.float32, mybir.dt.bfloat16, mybir.dt.uint32
    ALU, ACT = mybir.AluOpType, mybir.ActivationFunctionType

    ctx = ExitStack()
    with ctx:
        def sb(name, shape, dt=fp32):
            return ctx.enter_context(nc.sbuf_tensor(name, shape, dt))

        def sem(name):
            return ctx.enter_context(nc.semaphore(name))

        X = sb("X", [P, NB, TPB, P])
        G_even = sb("G_even", [P, NB, TPB, P])
        G_odd = sb("G_odd", [P, NB, TPB, P])
        G_last = sb("G_last", [P, NB, TPB, P])
        HT = sb("HT", [P, NB, BLK])
        resident = sb("resident", [P, NB, TPB, BLK])
        ring = sb("ring", [P, SLOTS, TPB, BLK])
        pack = sb("pack", [P, PACK])
        colsum = sb("colsum", [P, TPB, BLK])
        rows_T = sb("rows_T", [P, BLK])
        gate_z = colsum[:, 2, :]
        cand = colsum[:, 3, :]
        nat = sb("nat", [P, TPB, P])
        hn = sb("hn", [P, TPB, P])
        gate_r = hn[:, :, :].rearrange("p t f -> p (t f)")
        hTs = sb("hTs", [P, BLK])
        stats = sb("stats", [P, TPB, 6])
        meanvar = sb("meanvar", [P, TPB, 2])
        std = sb("std", [P, TPB])
        rstd = sb("rstd", [P, TPB])
        degree = sb("degree", [P, NB, TPB])
        deg_pair = sb("deg_pair", [P, 2, TPB])
        deg_root = sb("deg_root", [P, 2, TPB])
        inv_root = sb("inv_root", [P, NB, 2, TPB])
        ssum = sb("ssum", [P, TPB])
        norm = sb("norm", [P, TPB])
        neg_sq = sb("neg_sq", [P, NT])
        sq_aug = colsum[0:3, :, :].bitcast(bf16).rearrange("p t (b n) -> p (t b) n", n=BLK)
        part_hi = sb("part_hi", [3, BLK], bf16)
        part_mid = sb("part_mid", [3, BLK], bf16)
        rest = sb("rest", [3, BLK])
        mixed = sb("mixed", [3, BLK])
        ones3 = sb("ones3", [3, P], bf16)
        halves = sb("halves", [P, 3])
        ones = sb("ones", [P, 1])
        eps_ln = sb("eps_ln", [P, 1])
        eps_d2 = sb("eps_d2", [P, 1])
        gate_bias = sb("gate_bias", [P, 2])
        best = rows_T[:, 0:NT * 8].rearrange("p (t e) -> p t e", e=8)
        best_at = sb("best_at", [P, NT, 8], u32)
        picks = sb("picks", [P, GSLOTS, TOPK], u32)
        simil = sb("simil", [P, NT, TOPK])
        deg2 = sb("deg2", [P, NT])
        root2 = sb("root2", [P, NT])
        d2inv = sb("d2inv", [P, NT])
        ps = ctx.enter_context(nc.psum_tensor("ps", [P, 8, BLK], fp32))
        TB, GB, AUX = 2, 3, 4
        scores = [G_even, G_odd]
        landing = G_odd[:, :, :, :]
        near = G_even

        w = lambda i: pack[:, i * P:(i + 1) * P]
        col = lambda i: pack[:, 16 * P + i:16 * P + i + 1]
        ident = w(IDENT)
        flat = lambda t, b: t[:, b, :, :].rearrange("p t f -> p (t f)")

        pack_loaded, consts_set = sem("pack_loaded"), sem("consts_set")
        x_loaded = [sem(f"x_loaded{b}") for b in range(NB)]
        res_loaded = sem("res_loaded")
        at_loaded = [sem(f"at_loaded{s}") for s in range(SLOTS)]
        used, summed = sem("used"), sem("summed")
        res_summed = sem("res_summed")
        acc_full, rowsT_ready, nat_full = sem("acc_full"), sem("rowsT_ready"), sem("nat_full")
        stats_ready, std_ready, hn_ready = sem("stats_ready"), sem("std_ready"), sem("hn_ready")
        hT_full, hTs_ready, g_full, g_ready = sem("hT_full"), sem("hTs_ready"), sem("g_full"), sem("g_ready")
        raw_full, raw_ready = sem("raw_full"), sem("raw_ready")
        colsum_ready, degree_full = sem("colsum_ready"), sem("degree_full")
        pair_ready, root_ready, inv_ready = sem("pair_ready"), sem("root_ready"), sem("inv_ready")
        v_ready, ss_ready, ssmax_ready, norm_ready = sem("v_ready"), sem("ss_ready"), sem("ssmax_ready"), sem("norm_ready")
        gates_full, rz_ready, t_ready, n_ready, u_ready = (
            sem("gates_full"), sem("rz_ready"), sem("t_ready"), sem("n_ready"), sem("u_ready"))
        z_ready, zT_full, z2_ready, sqrow_full, aug_ready = (
            sem("z_ready"), sem("zT_full"), sem("z2_ready"), sem("sqrow_full"), sem("aug_ready"))
        ztile_ready, half_full, half_out, scanned = sem("ztile_ready"), sem("half_full"), sem("half_out"), sem("scanned")
        negsq_ready = sem("negsq_ready")
        clamp_ready, dist_ready, simil_ready, deg2_ready, root2_ready = (
            sem("clamp_ready"), sem("dist_ready"), sem("simil_ready"), sem("deg2_ready"), sem("root2_ready"))
        last_ready, rows_stored = sem("last_ready"), sem("rows_stored")
        gathered = [sem(f"gathered{s}") for s in range(GSLOTS)]
        picks_ready = sem("picks_ready")
        weighted, x_final, out_stored = sem("weighted"), sem("x_final"), sem("out_stored")
        bias_ready, dve_step, act_step = sem("bias_ready"), sem("dve_step"), sem("act_step")

        SPARES = 8
        spare = sb("spare", [P, 3 * SPARES])
        holds = [0]

        def hold(eng, semaphore, value):
            eng.wait_ge(semaphore, value)
            if isinstance(value, int):
                return
            holds[0] += 1
            at = lambda e: spare[:, e * SPARES + holds[0] % SPARES:e * SPARES + holds[0] % SPARES + 1]
            if eng is nc.vector:
                nc.vector.memset(at(0), 0.0)
            elif eng is nc.scalar:
                nc.scalar.activation(at(1), ones[:, :], ACT.Copy)
            else:
                nc.gpsimd.tensor_tensor(at(2), ones[:, :], ones[:, :], ALU.add)

        block = ctx.enter_context(nc.Block())

        @block.sync
        def _(sp):
            sp.dma_start(pack[:, :], pack_in).then_inc(pack_loaded, 16)
            for b in range(NB):
                sp.dma_start(X[:, b, :, :], x_in[:, b, :, :]).then_inc(x_loaded[b], 16)

            def load_block(q, first):
                if first:
                    if not isinstance(q, int):
                        sp.wait_ge(res_loaded, q * 16)
                    sp.dma_start(resident[:, q, :, :], at_in[q, 0, :, :, :]).then_inc(res_loaded, 16)
                for m in range(1, NB):
                    s, _u = streamed(m)
                    free = previous_use(q, m)
                    if not isinstance(free, int) or free > 0:
                        sp.wait_ge(used, free)
                        if first:
                            sp.wait_ge(summed, free)
                    sp.dma_start(ring[:, s, :, :], at_in[q % NB, m, :, :, :]).then_inc(at_loaded[s], 16)

            load_block(0, True)
            with sp.Fori(1, NB) as q:
                load_block(q, True)
            sp.wait_ge(summed, STREAMED * NB)
            with sp.Fori(NB, LAYERS * NB) as q:
                load_block(q, False)

        @block.tensor
        def _(pe):
            mm = nc.tensor.matmul

            def main_block(p, b, after):
                q = NB * p + b
                G = (G_even, G_odd, G_even, G_odd, G_last)[p]
                acc = ps[:, b % 2, :]
                if p or not isinstance(b, int):
                    pe.wait_ge(rowsT_ready, q - 1)
                if p == 0:
                    if isinstance(b, int):
                        pe.wait_ge(hTs_ready, 1)
                    mm(acc, w(W_SELF), HT[:, b, :], start=True, stop=False)
                for m in range(NB):
                    if isinstance(b, int):
                        if p < 4:
                            pe.wait_ge(g_ready, NB * p + m + 1)
                        elif m == 0:
                            pe.wait_ge(last_ready, 1)
                    if m == 0:
                        if p == 0:
                            pe.wait_ge(res_loaded, 16 * (b + 1))
                        src = resident[:, b, :, :]
                    else:
                        s, _u = streamed(m)
                        pe.wait_ge(at_loaded[s], loaded_value(q, m))
                        src = ring[:, s, :, :]
                    for k in range(TPB if m else TPB - 1):
                        last = mm(acc, G[:, m, k, :], src[:, k, :],
                                  start=(p > 0 and m == 0 and k == 0), stop=False)
                    if m:
                        last.then_inc(used, 1)
                    if m == NB - 1:
                        mm(acc, G[:, 0, TPB - 1, :], resident[:, b, TPB - 1, :],
                           start=False, stop=True).then_inc(acc_full, 1)
                    if m in after:
                        after[m]()

            def to_natural(p, b):
                q = NB * p + b
                if p == 2:
                    pe.wait_ge(u_ready, b + 1)
                    src = cand
                else:
                    pe.wait_ge(rowsT_ready, q + 1)
                    src = rows_T
                if p == 3 and not (isinstance(b, int) and b == 0):
                    pe.wait_ge(z2_ready, b)
                elif p == 4:
                    if not (isinstance(b, int) and b == 0):
                        pe.wait_ge(x_final, b)
                else:
                    pe.wait_ge(hTs_ready, q + NB)
                for n in range(TPB):
                    last = nc.tensor.transpose(ps[:, TB, n * P:(n + 1) * P], src[:, n * P:(n + 1) * P], ident)
                last.then_inc(nat_full, 1)

            def h_transposes(h):
                pe.wait_ge(hn_ready, h + 1)
                if not (isinstance(h, int) and h == 0):
                    pe.wait_ge(hTs_ready, h)
                for n in range(TPB):
                    last = nc.tensor.transpose(ps[:, TB, n * P:(n + 1) * P], hn[:, n, :], ident)
                last.then_inc(hT_full, 1)

            def operand(h, weight, raw=None):
                pe.wait_ge(hTs_ready, h + 1)
                if not (isinstance(h, int) and h == 0):
                    pe.wait_ge(g_ready, h)
                for n in range(TPB):
                    last = mm(ps[:, GB, n * P:(n + 1) * P], hTs[:, n * P:(n + 1) * P], w(weight),
                              start=True, stop=True)
                last.then_inc(g_full, 1)
                if raw is not None:
                    for n in range(TPB):
                        last = mm(ps[:, AUX, n * P:(n + 1) * P], hTs[:, n * P:(n + 1) * P], w(raw),
                                  start=True, stop=True)
                    last.then_inc(raw_full, 1)

            def degree_sums(b):
                pe.wait_ge(colsum_ready, b + 1)
                if not (isinstance(b, int) and b == 0):
                    pe.wait_ge(pair_ready, b)
                for n in range(TPB):
                    last = mm(ps[:, AUX, n:n + 1], colsum[:, 0, n * P:(n + 1) * P], ones[:, :],
                              start=True, stop=True)
                last.then_inc(degree_full, 1)

            def gates(b):
                pe.wait_ge(rowsT_ready, 2 * NB + b + 1)
                if isinstance(b, int) and b == 0:
                    pe.wait_ge(pair_ready, NB)
                else:
                    pe.wait_ge(raw_ready, b)
                for n, (wi, wh) in enumerate(((W_IR, W_HR), (W_IZ, W_HZ))):
                    mm(ps[:, AUX + n, :], w(wi), rows_T[:, :], start=True, stop=False)
                    mm(ps[:, AUX + n, :], w(wh), HT[:, b, :], start=False, stop=True)
                mm(ps[:, AUX + 2, :], w(W_IN), rows_T[:, :], start=True, stop=True)
                mm(ps[:, AUX + 3, :], w(W_HN), HT[:, b, :], start=True, stop=True).then_inc(gates_full, 1)

            def z_transposes(b):
                pe.wait_ge(z_ready, b + 1)
                for n in range(TPB):
                    last = nc.tensor.transpose(ps[:, TB, n * P:(n + 1) * P], nat[:, n, :], ident)
                last.then_inc(zT_full, 1)

            def square_row(b):
                pe.wait_ge(z2_ready, b + 1)
                if isinstance(b, int) and b == 0:
                    pe.wait_ge(g_ready, 4 * NB)
                else:
                    pe.wait_ge(aug_ready, b)
                mm(ps[0:3, GB, :], halves[:, :], hTs[:, :], start=True, stop=True).then_inc(sqrow_full, 1)

            def epilogue(p, b):
                h = NB * (p + 1) + b
                if p == 0:
                    return {0: lambda: (degree_sums(b), to_natural(p, b)), 3: lambda: h_transposes(h),
                            5: lambda: operand(h, W_L1)}
                if p == 1:
                    return {0: lambda: to_natural(p, b), 4: lambda: h_transposes(h),
                            5: lambda: operand(h, W_MSG)}
                if p == 2:
                    return {0: lambda: gates(b), 2: lambda: to_natural(p, b), 4: lambda: h_transposes(h),
                            5: lambda: operand(h, W_LAP1, W_LAP2)}
                if p == 3:
                    return {0: lambda: to_natural(p, b), 2: lambda: z_transposes(b), 4: lambda: square_row(b)}
                return {0: lambda: to_natural(p, b)}

            def finish(p, b):
                for step in epilogue(p, b).values():
                    step()

            pe.wait_ge(pack_loaded, 16)
            pe.wait_ge(consts_set, 1)
            for b in range(NB):
                h_transposes(b)
                operand(b, W_NEIGH)

            for p in range(4):
                main_block(p, 0, epilogue(p - 1, NB - 1) if p else {})
                with pe.Fori(1, NB) as b:
                    main_block(p, b, epilogue(p, b - 1))
            finish(3, NB - 1)

            pe.wait_ge(aug_ready, NB)

            def pair_rows(t, odd):
                pe.wait_ge(ztile_ready, t + 1)
                zt = (gate_r, hTs)[odd][:, 0:P]
                for half in range(2):
                    if not (isinstance(t, int) and t == 0):
                        pe.wait_ge(half_out, 2 * t + half - 1)
                    for c in range(4 * half, 4 * half + 4):
                        mm(ps[:, c, :], zt, HT[:, c, :], start=True, stop=False)
                        last = mm(ps[:, c, :], ones3[:, :], sq_aug[:, c, :], start=False, stop=True)
                    last.then_inc(half_full, 1)

            pair_rows(0, 0)
            pair_rows(1, 1)
            with pe.Fori(1, NT // 2) as pair:
                t = 2 * pair
                pair_rows(t, 0)
                pair_rows(t + 1, 1)
            pe.wait_ge(half_out, 2 * NT)

            main_block(4, 0, {})
            with pe.Fori(1, NB) as b:
                main_block(4, b, epilogue(4, b - 1))
            finish(4, NB - 1)

        @block.scalar
        def _(act):
            def f(out_ap, in_ap, func, **k):
                return nc.scalar.activation(out_ap, in_ap, func, **k)

            def copy_out(p, b):
                q = NB * p + b
                act.wait_ge(acc_full, q + 1)
                if p or not isinstance(b, int):
                    act.wait_ge(nat_full, q)
                if p == 0:
                    ins = f(rows_T[:, :], ps[:, b % 2, :], ACT.Relu, bias=col(C_L0))
                elif p == 2:
                    ins = f(rows_T[:, :], ps[:, b % 2, :], ACT.Relu, bias=col(C_MSG))
                else:
                    ins = f(rows_T[:, :], ps[:, b % 2, :], ACT.Copy)
                ins.then_inc(rowsT_ready, 1)

            def make_h(h, b, p):
                act.wait_ge(stats_ready, h + 1)
                f(std[:, :], meanvar[:, :, 1], ACT.Sqrt, bias=eps_ln[:, :]).then_inc(std_ready, 1)
                act.wait_ge(hT_full, h + 1)
                if p in (0, 2):
                    f(HT[:, b, :], ps[:, TB, :], ACT.Relu)
                f(hTs[:, :], ps[:, TB, :], ACT.Relu).then_inc(hTs_ready, 1)
                act.wait_ge(g_full, h + 1)
                G = (G_even, G_odd, G_even, G_odd)[p]
                if p in (0, 2):
                    f(flat(G, b), ps[:, GB, :], ACT.Copy).then_inc(g_ready, 1)
                else:
                    if p == 1:
                        hold(act, inv_ready, b + 1)
                    for n in range(TPB):
                        last = f(G[:, b, n, :], ps[:, GB, n * P:(n + 1) * P], ACT.Copy,
                                 scale=inv_root[:, b, 1 if p == 1 else 0, n:n + 1])
                    last.then_inc(g_ready, 1)
                if p == 3:
                    act.wait_ge(raw_full, b + 1)
                    f(flat(G_last, b), ps[:, AUX, :], ACT.Copy).then_inc(raw_ready, 1)

            def epilogue(p, b):
                h = NB * (p + 1) + b
                copy_out(p, b)
                if p == 0:
                    act.wait_ge(pair_ready, b + 1)
                    f(deg_root[:, :, :], deg_pair[:, :, :], ACT.Sqrt).then_inc(root_ready, 1)
                if p == 1:
                    act.wait_ge(v_ready, b + 1)
                    for n in range(TPB):
                        last = f(gate_r[:, n * P:(n + 1) * P], nat[:, n, :], ACT.Square,
                                 accum_out=ssum[:, n:n + 1])
                    last.then_inc(ss_ready, 1)
                    act.wait_ge(ssmax_ready, b + 1)
                    f(norm[:, :], ssum[:, :], ACT.Sqrt).then_inc(norm_ready, 1)
                if p == 2:
                    act.wait_ge(gates_full, b + 1)
                    act.wait_ge(bias_ready, 1)
                    f(gate_r[:, :], ps[:, AUX, :], ACT.Sigmoid, bias=gate_bias[:, 0:1])
                    f(gate_z[:, :], ps[:, AUX + 1, :], ACT.Sigmoid, bias=gate_bias[:, 1:2]).then_inc(rz_ready, 1)
                    act.wait_ge(t_ready, b + 1)
                    f(hTs[:, :], cand[:, :], ACT.Tanh, bias=col(C_IN)).then_inc(n_ready, 1)
                if p == 3:
                    act.wait_ge(z_ready, b + 1)
                    for n in range(TPB):
                        last = f(gate_r[:, n * P:(n + 1) * P], nat[:, n, :], ACT.Square,
                                 accum_out=neg_sq[:, bass.ds(b * TPB + n, 1)])
                    act.wait_ge(zT_full, b + 1)
                    f(HT[:, b, :], ps[:, TB, :], ACT.Copy)
                    f(hTs[:, :], ps[:, TB, :], ACT.Square).then_inc(z2_ready, 1)
                    return
                if p < 3:
                    make_h(h, b, p + 1)

            act.wait_ge(pack_loaded, 16)
            act.wait_ge(consts_set, 1)
            for b in range(NB):
                make_h(b, b, 0)
            for p in range(4):
                epilogue(p, 0)
                with act.Fori(1, NB) as b:
                    epilogue(p, b)

            act.wait_ge(negsq_ready, 1)
            act.wait_ge(aug_ready, NB)

            def stage_tile(t, odd):
                if isinstance(t, int) and t < 2:
                    act.wait_ge(z2_ready, NB)
                else:
                    act.wait_ge(half_full, 2 * t - 2)
                f((gate_r, hTs)[odd][:, 0:P], HT[:, :, :].rearrange("p b (t n) -> p (b t) n", n=P)[:, t, :],
                  ACT.Copy).then_inc(ztile_ready, 1)

            def pair_out(t, odd):
                if not (isinstance(t, int) and t < 2):
                    act.wait_ge(scanned, t - 1)
                for half in range(2):
                    hold(act, half_full, 2 * t + half + 1)
                    f(scores[odd][:, 4 * half:4 * half + 4, :, :].rearrange("p b t f -> p (b t f)"),
                      ps[:, 4 * half:4 * half + 4, :].rearrange("p c n -> p (c n)"), ACT.Identity,
                      scale=2.0, bias=neg_sq[:, bass.ds(t, 1)]).then_inc(half_out, 1)

            stage_tile(0, 0)
            stage_tile(1, 1)
            def two_tiles(t):
                for odd in range(2):
                    pair_out(t + odd, odd)
                    stage_tile(t + odd + 2, odd)

            two_tiles(0)
            with act.Fori(1, NT // 2 - 1) as pair:
                two_tiles(2 * pair)
            pair_out(NT - 2, 0)
            pair_out(NT - 1, 1)

            act.wait_ge(clamp_ready, 1)
            f(simil[:, :, :], simil[:, :, :], ACT.Sqrt, scale=-1.0, bias=eps_d2[:, :]).then_inc(dist_ready, 1)
            act.wait_ge(dist_ready, 1)
            f(simil[:, :, :], simil[:, :, :], ACT.Exp, scale=-0.5).then_inc(simil_ready, 1)
            act.wait_ge(deg2_ready, 1)
            f(root2[:, :], deg2[:, :], ACT.Sqrt).then_inc(root2_ready, 1)

            def last_block(b):
                copy_out(4, b)
                act.wait_ge(x_final, b + 1)
                act.dma_start(out[b, :, :, :], X[:, b, :, :]).then_inc(out_stored, 16)

            last_block(0)
            with act.Fori(1, NB) as b:
                last_block(b)
            act.wait_ge(out_stored, 16 * NB)

        @block.vector
        def _(dve):
            v = nc.vector
            own = Steps(dve, dve_step)

            def rows_of(t, b):
                return flat(t, b)

            def layernorm(h, b):
                for n in range(TPB):
                    last = v.bn_stats(stats[:, n, :], X[:, b, n, :])
                own.add(last)
                hold(dve, dve_step, own.value())
                for n in range(TPB):
                    last = v.bn_aggr(meanvar[:, n, :], stats[:, n, :])
                last.then_inc(stats_ready, 1)
                dve.wait_ge(std_ready, h + 1)
                own.add(v.reciprocal(rstd[:, :], std[:, :]))
                own.settle()
                if not (isinstance(h, int) and h == 0):
                    dve.wait_ge(hT_full, h)
                for n in range(TPB):
                    last = v.tensor_scalar(hn[:, n, :], X[:, b, n, :], meanvar[:, n, 0:1], rstd[:, n:n + 1],
                                           ALU.subtract, ALU.mult)
                last.then_inc(hn_ready, 1)

            def sum_pieces(b, after):
                if not (isinstance(b, int) and b == 0):
                    dve.wait_ge(degree_full, b)
                dve.wait_ge(res_loaded, 16 * (b + 1))
                last = v.tensor_copy(colsum[:, :, :], resident[:, b, :, :])
                own.add(last)
                for m in range(NB):
                    if m:
                        s, _u = streamed(m)
                        dve.wait_ge(at_loaded[s], loaded_value(b, m))
                        if m == 1:
                            own.settle()
                        else:
                            dve.wait_ge(summed, STREAMED * b + m - 1)
                        v.tensor_tensor(colsum[:, :, :], colsum[:, :, :], ring[:, s, :, :],
                                        ALU.add).then_inc(summed, 1)
                    if m in after:
                        after[m]()
                dve.wait_ge(summed, STREAMED * (b + 1))
                own.add(v.tensor_tensor(colsum[:, 0:2, :], colsum[:, 0:2, :], colsum[:, 2:4, :], ALU.add))
                own.settle()
                v.tensor_tensor(colsum[:, 0, :], colsum[:, 0, :], colsum[:, 1, :],
                                ALU.add).then_inc(colsum_ready, 1)

            def degrees(b):
                dve.wait_ge(degree_full, b + 1)
                if not (isinstance(b, int) and b == 0):
                    dve.wait_ge(root_ready, b)
                v.tensor_copy(degree[:, b, :], ps[:, AUX, 0:TPB])
                v.tensor_copy(deg_pair[:, 0, :], ps[:, AUX, 0:TPB])
                v.tensor_scalar(deg_pair[:, 1, :], ps[:, AUX, 0:TPB], 1.0, None, ALU.add).then_inc(pair_ready, 1)
                dve.wait_ge(root_ready, b + 1)
                v.reciprocal(inv_root[:, b, :, :], deg_root[:, :, :]).then_inc(inv_ready, 1)

            def add_rows(p, b):
                dve.wait_ge(nat_full, NB * p + b + 1)
                own.add(v.tensor_tensor(rows_of(X, b), rows_of(X, b), ps[:, TB, :], ALU.add))
                hold(dve, dve_step, own.value())

            def l1_rows(b):
                q = NB + b
                dve.wait_ge(nat_full, q + 1)
                own.add(v.tensor_tensor(nat[:, :, :].rearrange("p t f -> p (t f)"), rows_of(G_odd, b),
                                        ps[:, TB, :], ALU.add))
                own.settle()
                for n in range(TPB):
                    last = v.scalar_tensor_tensor(nat[:, n, :], nat[:, n, :], inv_root[:, b, 1, n:n + 1],
                                                  w(ROW_L1), ALU.mult, ALU.add)
                last.then_inc(v_ready, 1)
                dve.wait_ge(ss_ready, b + 1)
                v.tensor_scalar(ssum[:, :], ssum[:, :], 1e-24, None, ALU.max).then_inc(ssmax_ready, 1)
                dve.wait_ge(norm_ready, b + 1)
                own.add(v.reciprocal(rstd[:, :], norm[:, :]))
                own.settle()
                for n in range(TPB):
                    last = v.scalar_tensor_tensor(X[:, b, n, :], nat[:, n, :], rstd[:, n:n + 1], X[:, b, n, :],
                                                  ALU.mult, ALU.add)
                own.add(last)
                hold(dve, dve_step, own.value())

            def gru(b):
                dve.wait_ge(rz_ready, b + 1)
                own.add(v.scalar_tensor_tensor(cand[:, :], ps[:, AUX + 3, :], col(C_HN), gate_r[:, :],
                                               ALU.add, ALU.mult))
                own.settle()
                v.tensor_tensor(cand[:, :], cand[:, :], ps[:, AUX + 2, :], ALU.add).then_inc(t_ready, 1)
                dve.wait_ge(n_ready, b + 1)
                own.add(v.tensor_tensor(cand[:, :], HT[:, b, :], hTs[:, :], ALU.subtract))
                own.settle()
                own.add(v.tensor_tensor(cand[:, :], cand[:, :], gate_z[:, :], ALU.mult))
                own.settle()
                v.tensor_tensor(cand[:, :], cand[:, :], hTs[:, :], ALU.add).then_inc(u_ready, 1)

            def lap_rows(b):
                dve.wait_ge(nat_full, 3 * NB + b + 1)
                for n in range(TPB):
                    last = v.scalar_tensor_tensor(nat[:, n, :], ps[:, TB, n * P:(n + 1) * P],
                                                  inv_root[:, b, 0, n:n + 1], w(ROW_LAP1), ALU.mult, ALU.add)
                own.add(last)
                own.settle()
                z = nat[:, :, :].rearrange("p t f -> p (t f)")
                v.scalar_tensor_tensor(z, z, 0.1, z, ALU.mult, ALU.max).then_inc(z_ready, 1)
                dve.wait_ge(sqrow_full, b + 1)
                row = ps[0:3, GB, :]
                own.add(v.tensor_copy(part_hi[:, :], row))
                own.settle()
                own.add(v.tensor_tensor(rest[:, :], row, part_hi[:, :], ALU.subtract))
                own.settle()
                own.add(v.tensor_copy(part_mid[:, :], rest[:, :]))
                own.settle()
                own.add(v.tensor_tensor(rest[:, :], rest[:, :], part_mid[:, :], ALU.subtract))
                own.add(v.tensor_scalar(mixed[:, :], part_hi[:, :], pack[0:3, 0:1], None, ALU.mult))
                own.settle()
                own.add(v.scalar_tensor_tensor(mixed[:, :], part_mid[:, :], pack[0:3, 1:2], mixed[:, :],
                                               ALU.mult, ALU.add))
                own.settle()
                v.scalar_tensor_tensor(sq_aug[:, b, :], rest[:, :], pack[0:3, 2:3], mixed[:, :],
                                       ALU.mult, ALU.add).then_inc(aug_ready, 1)

            def epilogue(p, b):
                h = NB * (p + 1) + b
                if p == 1:
                    l1_rows(b)
                elif p == 2:
                    gru(b)
                    add_rows(p, b)
                elif p == 3:
                    lap_rows(b)
                if p in (1, 2):
                    layernorm(h, b)

            def first_steps(b):
                return {0: lambda: degrees(b), 1: lambda: add_rows(0, b), 2: lambda: layernorm(NB + b, b)}

            dve.wait_ge(pack_loaded, 16)
            v.tensor_tensor(gate_bias[:, :], pack[:, 16 * P + C_IR:16 * P + C_IR + 2],
                            pack[:, 16 * P + C_HR:16 * P + C_HR + 2], ALU.add).then_inc(bias_ready, 1)
            for b in range(NB):
                dve.wait_ge(x_loaded[b], 16)
                layernorm(b, b)

            sum_pieces(0, {})
            at, per = own.base + own.n, SUM_STEPS
            with dve.Fori(1, NB) as b:
                own.turn(at + (b - 1) * per)
                sum_pieces(b, first_steps(b - 1))
                assert own.n == per, own.n
            own.turn(at + (NB - 1) * per)
            for step in first_steps(NB - 1).values():
                step()
            for p in range(1, 4):
                epilogue(p, 0)
                at, per = own.base + own.n, EPI_STEPS[p]
                with dve.Fori(1, NB) as b:
                    own.turn(at + (b - 1) * per)
                    epilogue(p, b)
                    assert own.n == per, (p, own.n)
                own.turn(at + (NB - 1) * per)

            dve.wait_ge(z2_ready, NB)
            v.tensor_scalar(neg_sq[:, :], neg_sq[:, :], -1.0, None, ALU.mult).then_inc(negsq_ready, 1)

            def scan(t, odd):
                dve.wait_ge(half_out, 2 * t + 2)
                row = scores[odd][:, :, :, :].rearrange("p b t f -> p (b t f)")
                own.add(v.max(best[:, t, :], row))
                own.settle()
                v.max_index(best_at[:, t, :], best[:, t, :], row).then_inc(scanned, 1)

            for t in range(NT):
                scan(t, t % 2)

            dve.wait_ge(scanned, NT)
            v.tensor_scalar(simil[:, :, :], best[:, :, 0:TOPK], 0.0, None, ALU.min).then_inc(clamp_ready, 1)
            dve.wait_ge(simil_ready, 1)
            own.add(v.reduce_sum(deg2[:, :], simil[:, :, :], axis=mybir.AxisListType.X))
            own.settle()
            v.tensor_tensor(deg2[:, :], deg2[:, :], degree[:, :, :].rearrange("p b t -> p (b t)"),
                            ALU.add).then_inc(deg2_ready, 1)
            dve.wait_ge(root2_ready, 1)
            own.add(v.reciprocal(d2inv[:, :], root2[:, :]))
            own.settle()
            for t in range(NT):
                last = v.tensor_scalar(G_last[:, t // TPB, t % TPB, :], G_last[:, t // TPB, t % TPB, :],
                                       d2inv[:, t:t + 1], None, ALU.mult)
            last.then_inc(last_ready, 1)

            def weigh(b, k):
                dve.wait_ge(gathered[k], 16 * TOPK * (b + 1))
                slot, dst, t = landing[:, k, :, :], near[:, b, k, :], b * TPB + k
                own.add(v.tensor_scalar(dst, slot[:, 0, :], simil[:, t, 0:1], None, ALU.mult))
                for r in range(1, TOPK):
                    own.settle()
                    ins = v.scalar_tensor_tensor(dst, slot[:, r, :], simil[:, t, r:r + 1], dst,
                                                 ALU.mult, ALU.add)
                    if r < TOPK - 1:
                        own.add(ins)
                ins.then_inc(weighted, 1)

            def last_rows(b):
                for k in range(TPB):
                    weigh(b, k)
                dve.wait_ge(weighted, TPB * b + TPB)
                dve.wait_ge(nat_full, 4 * NB + b + 1)
                own.add(v.tensor_tensor(nat[:, :, :].rearrange("p t f -> p (t f)"), rows_of(near, b),
                                        ps[:, TB, :], ALU.add))
                own.settle()
                for n in range(TPB):
                    last = v.scalar_tensor_tensor(nat[:, n, :], nat[:, n, :],
                                                  d2inv[:, bass.ds(b * TPB + n, 1)],
                                                  w(ROW_LAP2), ALU.mult, ALU.add)
                own.add(last)
                own.settle()
                v.tensor_tensor(rows_of(X, b), rows_of(X, b), nat[:, :, :].rearrange("p t f -> p (t f)"),
                                ALU.add).then_inc(x_final, 1)

            last_rows(0)
            at, per = own.base + own.n, LAST_STEPS
            with dve.Fori(1, NB) as b:
                own.turn(at + (b - 1) * per)
                last_rows(b)
                assert own.n == per, own.n

        @block.gpsimd
        def _(pool):
            g = nc.gpsimd
            g.memset(ones3[:, :], 1.0)
            g.memset(halves[:, :], -0.5)
            g.memset(ones[:, :], 1.0)
            g.memset(eps_ln[:, :], 1e-5)
            g.memset(eps_d2[:, :], 1e-10).then_inc(consts_set, 1)

            pool.wait_ge(last_ready, 1)
            pool.dma_start(scaled_rows.rearrange("(b t p) f -> p (b t) f", t=TPB, p=P),
                           G_last.rearrange("p b t f -> p (b t) f")).then_inc(rows_stored, 16)
            pool.wait_ge(rows_stored, 16)

            def gather(t, k):
                if not (isinstance(t, int) and t < GSLOTS):
                    pool.wait_ge(weighted, t - GSLOTS + 1)
                g.tensor_copy(picks[:, k, :], best_at[:, t, 0:TOPK]).then_inc(picks_ready, 1)
                hold(pool, picks_ready, t + 1)
                for r in range(TOPK):
                    pool.indirect_dma_start(
                        out=landing[:, k, r, :], out_offset=None, in_=scaled_rows,
                        in_offset=bass.IndirectOffsetOnAxis(ap=picks[:, k, r:r + 1], axis=0),
                    ).then_inc(gathered[k], 16)

            for k in range(GSLOTS):
                gather(k, k)
            with pool.Fori(1, NT // GSLOTS) as turn:
                for k in range(GSLOTS):
                    gather(GSLOTS * turn + k, k)


SUM_STEPS = 5
EPI_STEPS = {1: 5, 2: 6, 3: 7}
LAST_STEPS = 14


def kernel(**inputs):
    import numpy as np
    import concourse.bacc as bacc
    from concourse.bass_utils import run_bass_kernel_spmd

    fp32 = mybir.dt.float32
    get = lambda n: np.asarray(inputs[n])
    x = np.ascontiguousarray(get("x").reshape(NB, TPB, P, P).transpose(2, 0, 1, 3))
    at = np.ascontiguousarray(get("adj").reshape(NB, BLK, NB, TPB, P).transpose(0, 2, 4, 3, 1))
    w0, w1, wm = get("L0_gnn_W"), get("L1_gnn_W"), get("L2_gnn_W_msg")
    wi, wh = get("L2_gnn_W_ih"), get("L2_gnn_W_hh")
    bi, bh = get("L2_gnn_b_ih").reshape(3, P), get("L2_gnn_b_hh").reshape(3, P)
    mats = [np.eye(P, dtype=np.float32), w0[:, :P].T, w0[:, P:].T, w1.T, wm.T]
    mats += [wi[g * P:(g + 1) * P].T for g in range(3)] + [wh[g * P:(g + 1) * P].T for g in range(3)]
    mats += [get("L3_gnn_W1"), get("L3_gnn_W2")]
    mats += [np.broadcast_to(get(n), (P, P)) for n in ("L1_gnn_b", "L3_gnn_b1", "L3_gnn_b2")]
    cols = [get("L0_gnn_b"), get("L2_gnn_b_msg"), bi[0], bi[1], bi[2], bh[0], bh[1], bh[2]]
    pack = np.ascontiguousarray(np.concatenate(mats + [c.reshape(P, 1) for c in cols], axis=1))

    nc = bacc.Bacc("TRN2", target_bir_lowering=False, num_devices=1, dynamic_dma_scratch_size=8192)
    arrays = {"x_rows": x, "adj_t": at, "packed": pack}
    aps = [nc.dram_tensor(n, a.shape, fp32, kind="ExternalInput").ap() for n, a in arrays.items()]
    scaled_rows = nc.dram_tensor("scaled_rows", (N, P), fp32, kind="Internal").ap()
    out = nc.dram_tensor("out_rows", (NB, P, TPB, P), fp32, kind="ExternalOutput").ap()
    gnn_stack(nc, *aps, scaled_rows, out)
    r = run_bass_kernel_spmd(nc, [arrays], core_ids=[0])
    got = r.results[0]["out_rows"]
    return np.ascontiguousarray(got.transpose(0, 2, 1, 3)).reshape(N, P)
```

```python
import concourse.bass as bass
from concourse import mybir
from contextlib import ExitStack

P = 128
N = 4096
BLK = 512
TPB = BLK // P
NB = N // BLK
NT = N // P
LAYERS = 5
UK = 2
UNITS = N // P // UK
SLOTS = 8
STAGED = 4
TOPK = 4
GSLOTS = 4

(IDENT, W_SELF, W_NEIGH, W_L1, W_MSG, W_IR, W_IZ, W_IN, W_HR, W_HZ, W_HN, W_LAP1, W_LAP2,
 ROW_L1, ROW_LAP1, ROW_LAP2) = range(16)
(C_L0, C_MSG, C_IR, C_IZ, C_IN, C_HR, C_HZ, C_HN) = range(8)
PACK = 16 * P + 8


class Steps:

    def __init__(self, eng, sem):
        self.eng, self.sem, self.base, self.n = eng, sem, 0, 0

    def add(self, ins):
        ins.then_inc(self.sem, 1)
        self.n += 1

    def value(self):
        return self.base + self.n

    def settle(self):
        self.eng.wait_ge(self.sem, self.value())

    def turn(self, base):
        self.base, self.n = base, 0


def loaded_value(q, u):
    return 16 * (UNITS // SLOTS * q + u // SLOTS + 1)


def whole(u):
    return u % 4 == 3


def rank(u):
    return u - (u + 1) // 4


SPLITS = rank(UNITS)


def used_before(q, u):
    r = rank(u) - STAGED
    q, r = (q, r) if r >= 0 else (q - 1, r + SPLITS)
    return UNITS * q + r + r // 3 + 1


def split_count(q, u):
    return SPLITS * (q - NB) + rank(u) + 1


def gnn_stack(nc, x_in, at_in, pack_in, scaled_rows, out):
    fp32, bf16, u32 = mybir.dt.float32, mybir.dt.bfloat16, mybir.dt.uint32
    ALU, ACT = mybir.AluOpType, mybir.ActivationFunctionType

    ctx = ExitStack()
    with ctx:
        def sb(name, shape, dt=fp32):
            return ctx.enter_context(nc.sbuf_tensor(name, shape, dt))

        def sem(name):
            return ctx.enter_context(nc.semaphore(name))

        r32 = mybir.dt.float32r
        place = [(nc.sbuf_base + 31) // 32 * 32]

        def at(name, shape, dt, offset):
            return nc.alloc_sbuf_tensor_at(name, shape, dt, offset=offset)

        def take(name, kib):
            place[0] += kib * 1024
            ctx.enter_context(nc.sbuf_tensor(name, [P, kib * 256], fp32))
            return place[0] - kib * 1024

        even, odd_at = take("area_even", 32), take("area_odd", 32)
        G_hi = [at("G_even_hi", [P, NB, TPB, P], r32, even), at("G_odd_hi", [P, NB, TPB, P], r32, odd_at)]
        G_lo = [at("G_even_lo", [P, NB, TPB, P], r32, even + 16384),
                at("G_odd_lo", [P, NB, TPB, P], r32, odd_at + 16384)]
        G_first = at("G_first", [P, NB, TPB, P], fp32, even)
        scores = [at(f"scores{n}", [P, N], fp32, even + 16384 * n) for n in range(2)]
        near = at("near", [P, NB, TPB, P], fp32, even)
        landing = at("landing", [P, GSLOTS, TOPK, P], fp32, even + 16384)
        X = sb("X", [P, NB, TPB, P])
        G_last = sb("G_last", [P, NB, TPB, P])
        HT = sb("HT", [P, NB, BLK])
        ring = sb("ring", [P, SLOTS, UK, BLK])
        A_hi = sb("A_hi", [P, STAGED, UK, BLK], r32)
        A_lo = sb("A_lo", [P, STAGED, UK, BLK], r32)
        G_whole = sb("G_whole", [P, UNITS // 4, UK, P])
        pack = sb("pack", [P, PACK])
        colsum = sb("colsum", [P, TPB, BLK])
        gate_z = colsum[:, 2, :]
        cand = colsum[:, 3, :]
        rows_T = sb("rows_T", [P, BLK])
        gate_z = colsum[:, 2, :]
        cand = colsum[:, 3, :]
        nat = sb("nat", [P, TPB, P])
        hn = sb("hn", [P, TPB, P])
        gate_r = hn[:, :, :].rearrange("p t f -> p (t f)")
        hTs = sb("hTs", [P, BLK])
        stats = sb("stats", [P, TPB, 6])
        meanvar = sb("meanvar", [P, TPB, 2])
        std = sb("std", [P, TPB])
        rstd = sb("rstd", [P, TPB])
        degree = sb("degree", [P, NB, TPB])
        deg_pair = sb("deg_pair", [P, 2, TPB])
        deg_root = sb("deg_root", [P, 2, TPB])
        inv_root = sb("inv_root", [P, NB, 2, TPB])
        ssum = sb("ssum", [P, TPB])
        norm = sb("norm", [P, TPB])
        neg_sq = sb("neg_sq", [P, NT])
        sq_aug = colsum[0:3, :, :].bitcast(bf16).rearrange("p t (b n) -> p (t b) n", n=BLK)
        part_hi = sb("part_hi", [3, BLK], bf16)
        part_mid = sb("part_mid", [3, BLK], bf16)
        rest = sb("rest", [3, BLK])
        mixed = sb("mixed", [3, BLK])
        ones3 = sb("ones3", [3, P], bf16)
        halves = sb("halves", [P, 3])
        ones = sb("ones", [P, 1])
        eps_ln = sb("eps_ln", [P, 1])
        eps_d2 = sb("eps_d2", [P, 1])
        gate_bias = sb("gate_bias", [P, 2])
        best = rows_T[:, 0:NT * 8].rearrange("p (t e) -> p t e", e=8)
        best_at = sb("best_at", [P, NT, 8], u32)
        picks = sb("picks", [P, GSLOTS, TOPK], u32)
        simil = sb("simil", [P, NT, TOPK])
        deg2 = sb("deg2", [P, NT])
        root2 = sb("root2", [P, NT])
        d2inv = sb("d2inv", [P, NT])
        ps = ctx.enter_context(nc.psum_tensor("ps", [P, 8, BLK], fp32))
        TB, GB, AUX = 2, 3, 4

        w = lambda i: pack[:, i * P:(i + 1) * P]
        col = lambda i: pack[:, 16 * P + i:16 * P + i + 1]
        ident = w(IDENT)
        flat = lambda t, b: t[:, b, :, :].rearrange("p t f -> p (t f)")

        pack_loaded, consts_set = sem("pack_loaded"), sem("consts_set")
        x_loaded = [sem(f"x_loaded{b}") for b in range(NB)]
        at_loaded = [sem(f"at_loaded{s}") for s in range(SLOTS)]
        used, summed = sem("used"), sem("summed")
        upper_ready, lower_ready = sem("upper_ready"), sem("lower_ready")
        whole_ready = sem("whole_ready")
        rowsT_ready, nat_full = sem("rowsT_ready"), sem("nat_full")
        stats_ready, std_ready, hn_ready = sem("stats_ready"), sem("std_ready"), sem("hn_ready")
        hT_full, hTs_ready, g_full, g_ready = sem("hT_full"), sem("hTs_ready"), sem("g_full"), sem("g_ready")
        ghi_ready = sem("ghi_ready")
        raw_full, raw_ready = sem("raw_full"), sem("raw_ready")
        colsum_ready, degree_full = sem("colsum_ready"), sem("degree_full")
        pair_ready, root_ready, inv_ready = sem("pair_ready"), sem("root_ready"), sem("inv_ready")
        v_ready, ss_ready, ssmax_ready, norm_ready = sem("v_ready"), sem("ss_ready"), sem("ssmax_ready"), sem("norm_ready")
        gates_full, rz_ready, t_ready, n_ready, u_ready = (
            sem("gates_full"), sem("rz_ready"), sem("t_ready"), sem("n_ready"), sem("u_ready"))
        z_ready, zT_full, z2_ready, sqrow_full, aug_ready = (
            sem("z_ready"), sem("zT_full"), sem("z2_ready"), sem("sqrow_full"), sem("aug_ready"))
        ztile_ready, half_full, half_out, scanned = sem("ztile_ready"), sem("half_full"), sem("half_out"), sem("scanned")
        negsq_ready = sem("negsq_ready")
        clamp_ready, dist_ready, simil_ready, deg2_ready, root2_ready = (
            sem("clamp_ready"), sem("dist_ready"), sem("simil_ready"), sem("deg2_ready"), sem("root2_ready"))
        last_ready, lasthi_ready, lastlo_ready = sem("last_ready"), sem("lasthi_ready"), sem("lastlo_ready")
        rows_stored = sem("rows_stored")
        gathered = [sem(f"gathered{s}") for s in range(GSLOTS)]
        picks_ready = sem("picks_ready")
        weighted, x_final, out_stored = sem("weighted"), sem("x_final"), sem("out_stored")
        bias_ready, dve_step, act_step = sem("bias_ready"), sem("dve_step"), sem("act_step")

        SPARES = 8
        spare = sb("spare", [P, 3 * SPARES])
        holds = [0]

        def hold(eng, semaphore, value):
            eng.wait_ge(semaphore, value)
            if isinstance(value, int):
                return
            holds[0] += 1
            at = lambda e: spare[:, e * SPARES + holds[0] % SPARES:e * SPARES + holds[0] % SPARES + 1]
            if eng is nc.vector:
                nc.vector.memset(at(0), 0.0)
            elif eng is nc.scalar:
                nc.scalar.activation(at(1), ones[:, :], ACT.Copy)
            else:
                nc.gpsimd.tensor_tensor(at(2), ones[:, :], ones[:, :], ALU.add)

        block = ctx.enter_context(nc.Block())

        @block.sync
        def _(sp):
            sp.dma_start(pack[:, :], pack_in).then_inc(pack_loaded, 16)
            for b in range(NB):
                sp.dma_start(X[:, b, :, :], x_in[:, b, :, :]).then_inc(x_loaded[b], 16)

            def load_block(q):
                for u in range(UNITS):
                    last = UNITS * q + u - SLOTS
                    owner, lu = (q, u - SLOTS) if u >= SLOTS else (q - 1, u + UNITS - SLOTS)
                    first = isinstance(q, int) and last < UNITS * NB
                    if not isinstance(q, int) or last >= 0:
                        if first or whole(lu):
                            sp.wait_ge(used, last + 1)
                        if first:
                            sp.wait_ge(summed, last + 1)
                        elif not whole(lu):
                            sp.wait_ge(lower_ready, split_count(owner, lu))
                    sp.dma_start(ring[:, u % SLOTS, :, :], at_in[q % NB, u, :, :, :])\
                        .then_inc(at_loaded[u % SLOTS], 16)

            def load_first(q):
                for u in range(UNITS):
                    last = UNITS * q + u - SLOTS
                    sp.wait_ge(used, last + 1)
                    sp.wait_ge(summed, last + 1)
                    sp.dma_start(ring[:, u % SLOTS, :, :], at_in[q, u, :, :, :])\
                        .then_inc(at_loaded[u % SLOTS], 16)

            load_block(0)
            with sp.Fori(1, NB) as q:
                load_first(q)
            load_block(NB)
            with sp.Fori(NB + 1, LAYERS * NB) as q:
                load_block(q)

        @block.tensor
        def _(pe):
            mm = nc.tensor.matmul

            def first_block(b, after):
                acc = ps[:, b % 2, :]
                if isinstance(b, int):
                    pe.wait_ge(hTs_ready, 1)
                else:
                    pe.wait_ge(rowsT_ready, b - 1)
                mm(acc, w(W_SELF), HT[:, b, :], start=True, stop=False)
                for u in range(UNITS):
                    if isinstance(b, int) and u % 2 == 0:
                        pe.wait_ge(g_ready, u // 2 + 1)
                    pe.wait_ge(at_loaded[u % SLOTS], loaded_value(b, u))
                    for k in range(UK):
                        last = mm(acc, G_first[:, u // 2, u % 2 * UK + k, :], ring[:, u % SLOTS, k, :],
                                  start=False, stop=(u == UNITS - 1 and k == UK - 1))
                    last.then_inc(used, 1)
                    if u in after:
                        after[u]()

            def split_block(p, b, after):
                q = NB * p + b
                odd = 1 if p == 4 else p % 2
                acc = ps[:, b % 2, :]
                pe.wait_ge(rowsT_ready, q - 1)
                for u in range(UNITS):
                    m = u // 2
                    if isinstance(b, int):
                        if p == 4:
                            pe.wait_ge(lastlo_ready, m + 1)
                        elif whole(u):
                            pe.wait_ge(whole_ready, (p - 1) * (UNITS // 4) + u // 4 + 1)
                        else:
                            pe.wait_ge(g_ready, NB * p + m + 1)
                    if whole(u):
                        pe.wait_ge(at_loaded[u % SLOTS], loaded_value(q, u))
                    else:
                        pe.wait_ge(lower_ready, split_count(q, u))
                    for k in range(UK):
                        kk = u % 2 * UK + k
                        end = u == UNITS - 1 and k == UK - 1
                        if whole(u):
                            G = G_last[:, m, kk, :] if p == 4 else G_whole[:, u // 4, k, :]
                            last = mm(acc, G, ring[:, u % SLOTS, k, :], start=False, stop=end)
                        else:
                            hi, lo = A_hi[:, rank(u) % STAGED, k, :], A_lo[:, rank(u) % STAGED, k, :]
                            mm(acc, G_hi[odd][:, m, kk, :], hi, start=(u == 0 and k == 0), stop=False)
                            mm(acc, G_hi[odd][:, m, kk, :], lo, start=False, stop=False)
                            last = mm(acc, G_lo[odd][:, m, kk, :], hi, start=False, stop=end)
                    last.then_inc(used, 1)
                    if u in after:
                        after[u]()

            def to_natural(p, b):
                q = NB * p + b
                if p == 2:
                    pe.wait_ge(u_ready, b + 1)
                    src = cand
                else:
                    pe.wait_ge(rowsT_ready, q + 1)
                    src = rows_T
                if p == 3 and not (isinstance(b, int) and b == 0):
                    pe.wait_ge(z2_ready, b)
                elif p == 4:
                    if not (isinstance(b, int) and b == 0):
                        pe.wait_ge(x_final, b)
                else:
                    pe.wait_ge(hTs_ready, q + NB)
                for n in range(TPB):
                    last = nc.tensor.transpose(ps[:, TB, n * P:(n + 1) * P], src[:, n * P:(n + 1) * P], ident)
                last.then_inc(nat_full, 1)

            def h_transposes(h):
                pe.wait_ge(hn_ready, h + 1)
                if not (isinstance(h, int) and h == 0):
                    pe.wait_ge(hTs_ready, h)
                for n in range(TPB):
                    last = nc.tensor.transpose(ps[:, TB, n * P:(n + 1) * P], hn[:, n, :], ident)
                last.then_inc(hT_full, 1)

            def operand(h, weight, raw=None):
                pe.wait_ge(hTs_ready, h + 1)
                if not (isinstance(h, int) and h == 0):
                    pe.wait_ge(g_ready, h)
                for n in range(TPB):
                    last = mm(ps[:, GB, n * P:(n + 1) * P], hTs[:, n * P:(n + 1) * P], w(weight),
                              start=True, stop=True)
                last.then_inc(g_full, 1)
                if raw is not None:
                    for n in range(TPB):
                        last = mm(ps[:, AUX, n * P:(n + 1) * P], hTs[:, n * P:(n + 1) * P], w(raw),
                                  start=True, stop=True)
                    last.then_inc(raw_full, 1)

            def degree_sums(b):
                pe.wait_ge(colsum_ready, b + 1)
                if not (isinstance(b, int) and b == 0):
                    pe.wait_ge(pair_ready, b)
                for n in range(TPB):
                    last = mm(ps[:, AUX, n:n + 1], colsum[:, 0, n * P:(n + 1) * P], ones[:, :],
                              start=True, stop=True)
                last.then_inc(degree_full, 1)

            def gates(b):
                pe.wait_ge(rowsT_ready, 2 * NB + b + 1)
                if isinstance(b, int) and b == 0:
                    pe.wait_ge(pair_ready, NB)
                else:
                    pe.wait_ge(raw_ready, b)
                for n, (wi, wh) in enumerate(((W_IR, W_HR), (W_IZ, W_HZ))):
                    mm(ps[:, AUX + n, :], w(wi), rows_T[:, :], start=True, stop=False)
                    mm(ps[:, AUX + n, :], w(wh), HT[:, b, :], start=False, stop=True)
                mm(ps[:, AUX + 2, :], w(W_IN), rows_T[:, :], start=True, stop=True)
                mm(ps[:, AUX + 3, :], w(W_HN), HT[:, b, :], start=True, stop=True).then_inc(gates_full, 1)

            def z_transposes(b):
                pe.wait_ge(z_ready, b + 1)
                for n in range(TPB):
                    last = nc.tensor.transpose(ps[:, TB, n * P:(n + 1) * P], nat[:, n, :], ident)
                last.then_inc(zT_full, 1)

            def square_row(b):
                pe.wait_ge(z2_ready, b + 1)
                if isinstance(b, int) and b == 0:
                    pe.wait_ge(g_ready, 4 * NB)
                else:
                    pe.wait_ge(aug_ready, b)
                mm(ps[0:3, GB, :], halves[:, :], hTs[:, :], start=True, stop=True).then_inc(sqrow_full, 1)

            def steps(p, b):
                h = NB * (p + 1) + b
                natural = lambda: to_natural(p, b)
                layernormed = lambda: h_transposes(h)
                return ((lambda: (degree_sums(b), natural()), layernormed, lambda: operand(h, W_L1)),
                        (natural, layernormed, lambda: operand(h, W_MSG)),
                        (lambda: gates(b), natural, layernormed, lambda: operand(h, W_LAP1, W_LAP2)),
                        (natural, lambda: z_transposes(b), lambda: square_row(b)),
                        (natural,))[p]

            def over(at_units, p, b):
                return dict(zip(at_units, steps(p, b)))

            pe.wait_ge(pack_loaded, 16)
            pe.wait_ge(consts_set, 1)
            for b in range(NB):
                h_transposes(b)
                operand(b, W_NEIGH)

            first_block(0, {})
            with pe.Fori(1, NB) as b:
                first_block(b, over(PE_FIRST, 0, b - 1))
            for p in range(1, 4):
                split_block(p, 0, over(PE_TURN[p - 1], p - 1, NB - 1))
                with pe.Fori(1, NB) as b:
                    split_block(p, b, over(PE_AT[p], p, b - 1))
            for step in steps(3, NB - 1):
                step()

            pe.wait_ge(aug_ready, NB)

            def pair_rows(t, odd):
                pe.wait_ge(ztile_ready, t + 1)
                zt = (gate_r, hTs)[odd][:, 0:P]
                for half in range(2):
                    if not (isinstance(t, int) and t == 0):
                        pe.wait_ge(half_out, 2 * t + half - 1)
                    for c in range(4 * half, 4 * half + 4):
                        mm(ps[:, c, :], zt, HT[:, c, :], start=True, stop=False)
                        last = mm(ps[:, c, :], ones3[:, :], sq_aug[:, c, :], start=False, stop=True)
                    last.then_inc(half_full, 1)

            pair_rows(0, 0)
            pair_rows(1, 1)
            with pe.Fori(1, NT // 2) as pair:
                t = 2 * pair
                pair_rows(t, 0)
                pair_rows(t + 1, 1)
            pe.wait_ge(half_out, 2 * NT)

            split_block(4, 0, {})
            with pe.Fori(1, NB) as b:
                split_block(4, b, over(PE_AT[4], 4, b - 1))
            for step in steps(4, NB - 1):
                step()

        @block.scalar
        def _(act):
            def f(out_ap, in_ap, func, **k):
                return nc.scalar.activation(out_ap, in_ap, func, **k)

            def copy_out(p, b):
                q = NB * p + b
                act.wait_ge(used, UNITS * (q + 1))
                if p or not isinstance(b, int):
                    act.wait_ge(nat_full, q)
                if p == 0:
                    ins = f(rows_T[:, :], ps[:, b % 2, :], ACT.Relu, bias=col(C_L0))
                elif p == 2:
                    ins = f(rows_T[:, :], ps[:, b % 2, :], ACT.Relu, bias=col(C_MSG))
                else:
                    ins = f(rows_T[:, :], ps[:, b % 2, :], ACT.Copy)
                ins.then_inc(rowsT_ready, 1)

            def roots(h):
                act.wait_ge(stats_ready, h + 1)
                f(std[:, :], meanvar[:, :, 1], ACT.Sqrt, bias=eps_ln[:, :]).then_inc(std_ready, 1)

            def rectify(h, b, p):
                act.wait_ge(hT_full, h + 1)
                if p in (0, 2):
                    f(HT[:, b, :], ps[:, TB, :], ACT.Relu)
                f(hTs[:, :], ps[:, TB, :], ACT.Relu).then_inc(hTs_ready, 1)

            def operand_out(h, b, p):
                act.wait_ge(g_full, h + 1)
                if p == 0:
                    f(flat(G_first, b), ps[:, GB, :], ACT.Copy).then_inc(g_ready, 1)
                    return
                if p == 2:
                    last = f(flat(G_hi[0], b), ps[:, GB, :], ACT.Copy)
                else:
                    hold(act, inv_ready, b + 1)
                    for n in range(TPB):
                        last = f(G_hi[1][:, b, n, :], ps[:, GB, n * P:(n + 1) * P], ACT.Copy,
                                 scale=inv_root[:, b, 1 if p == 1 else 0, n:n + 1])
                last.then_inc(ghi_ready, 1)
                if p == 3:
                    act.wait_ge(raw_full, b + 1)
                    f(flat(G_last, b), ps[:, AUX, :], ACT.Copy).then_inc(raw_ready, 1)

            def degree_roots(b):
                act.wait_ge(pair_ready, b + 1)
                f(deg_root[:, :, :], deg_pair[:, :, :], ACT.Sqrt).then_inc(root_ready, 1)

            def squares(p, b):
                act.wait_ge(v_ready if p == 1 else z_ready, b + 1)
                for n in range(TPB):
                    last = f(gate_r[:, n * P:(n + 1) * P], nat[:, n, :], ACT.Square,
                             accum_out=ssum[:, n:n + 1] if p == 1 else neg_sq[:, bass.ds(b * TPB + n, 1)])
                if p == 1:
                    last.then_inc(ss_ready, 1)

            def norms(b):
                act.wait_ge(ssmax_ready, b + 1)
                f(norm[:, :], ssum[:, :], ACT.Sqrt).then_inc(norm_ready, 1)

            def sigmoids(b):
                act.wait_ge(gates_full, b + 1)
                act.wait_ge(bias_ready, 1)
                f(gate_r[:, :], ps[:, AUX, :], ACT.Sigmoid, bias=gate_bias[:, 0:1])
                f(gate_z, ps[:, AUX + 1, :], ACT.Sigmoid, bias=gate_bias[:, 1:2]).then_inc(rz_ready, 1)

            def candidate(b):
                act.wait_ge(t_ready, b + 1)
                f(hTs[:, :], cand, ACT.Tanh, bias=col(C_IN)).then_inc(n_ready, 1)

            def z_out(b):
                act.wait_ge(zT_full, b + 1)
                f(HT[:, b, :], ps[:, TB, :], ACT.Copy)
                f(hTs[:, :], ps[:, TB, :], ACT.Square).then_inc(z2_ready, 1)

            def send(b):
                act.wait_ge(x_final, b + 1)
                act.dma_start(out[b, :, :, :], X[:, b, :, :]).then_inc(out_stored, 16)

            def steps(p, b):
                h = NB * (p + 1) + b
                tail = (lambda: roots(h), lambda: rectify(h, b, p + 1), lambda: operand_out(h, b, p + 1))
                out_of = lambda: copy_out(p, b)
                return ((out_of, lambda: degree_roots(b), *tail),
                        (out_of, lambda: squares(1, b), lambda: norms(b), *tail),
                        (out_of, lambda: sigmoids(b), lambda: candidate(b), *tail),
                        (out_of, lambda: squares(3, b), lambda: z_out(b)),
                        (out_of, lambda: send(b)))[p]

            def over(at_units, p, b):
                return dict(zip(at_units, steps(p, b)))

            def upper_block(q, after):
                for u in range(UNITS):
                    if not whole(u):
                        act.wait_ge(at_loaded[u % SLOTS], loaded_value(q, u))
                        if not isinstance(q, int) or q > NB or rank(u) >= STAGED:
                            act.wait_ge(used, used_before(q, u))
                        f(A_hi[:, rank(u) % STAGED, :, :], ring[:, u % SLOTS, :, :],
                          ACT.Copy).then_inc(upper_ready, 1)
                    if u in after:
                        after[u]()

            act.wait_ge(pack_loaded, 16)
            act.wait_ge(consts_set, 1)
            for b in range(NB):
                roots(b)
                rectify(b, b, 0)
                operand_out(b, b, 0)
            for step in steps(0, 0):
                step()
            with act.Fori(1, NB - 1) as b:
                for step in steps(0, b):
                    step()
            for p in range(1, 4):
                upper_block(NB * p, over(ACT_TURN[p - 1], p - 1, NB - 1))
                with act.Fori(1, NB) as b:
                    upper_block(NB * p + b, over(ACT_AT[p], p, b - 1))
            for step in steps(3, NB - 1):
                step()

            act.wait_ge(negsq_ready, 1)
            act.wait_ge(aug_ready, NB)

            def stage_tile(t, odd):
                if isinstance(t, int) and t < 2:
                    act.wait_ge(z2_ready, NB)
                else:
                    act.wait_ge(half_full, 2 * t - 2)
                f((gate_r, hTs)[odd][:, 0:P], HT[:, :, :].rearrange("p b (t n) -> p (b t) n", n=P)[:, t, :],
                  ACT.Copy).then_inc(ztile_ready, 1)

            def pair_out(t, odd):
                if not (isinstance(t, int) and t < 2):
                    act.wait_ge(scanned, t - 1)
                for half in range(2):
                    hold(act, half_full, 2 * t + half + 1)
                    f(scores[odd][:, half * (N // 2):(half + 1) * (N // 2)],
                      ps[:, 4 * half:4 * half + 4, :].rearrange("p c n -> p (c n)"), ACT.Identity,
                      scale=2.0, bias=neg_sq[:, bass.ds(t, 1)]).then_inc(half_out, 1)

            stage_tile(0, 0)
            stage_tile(1, 1)
            def two_tiles(t):
                for odd in range(2):
                    pair_out(t + odd, odd)
                    stage_tile(t + odd + 2, odd)

            two_tiles(0)
            with act.Fori(1, NT // 2 - 1) as pair:
                two_tiles(2 * pair)
            pair_out(NT - 2, 0)
            pair_out(NT - 1, 1)

            act.wait_ge(clamp_ready, 1)
            f(simil[:, :, :], simil[:, :, :], ACT.Sqrt, scale=-1.0, bias=eps_d2[:, :]).then_inc(dist_ready, 1)
            act.wait_ge(dist_ready, 1)
            f(simil[:, :, :], simil[:, :, :], ACT.Exp, scale=-0.5).then_inc(simil_ready, 1)
            act.wait_ge(deg2_ready, 1)
            f(root2[:, :], deg2[:, :], ACT.Sqrt).then_inc(root2_ready, 1)

            for b in range(NB):
                act.wait_ge(last_ready, b + 1)
                f(flat(G_hi[1], b), flat(G_last, b), ACT.Copy).then_inc(lasthi_ready, 1)
            upper_block(4 * NB, {})
            with act.Fori(1, NB) as b:
                upper_block(4 * NB + b, over(ACT_AT[4], 4, b - 1))
            for step in steps(4, NB - 1):
                step()
            act.wait_ge(out_stored, 16 * NB)

        @block.vector
        def _(dve):
            v = nc.vector
            own = Steps(dve, dve_step)

            def rows_of(t, b):
                return flat(t, b)

            def statistics(h, b):
                for n in range(TPB):
                    last = v.bn_stats(stats[:, n, :], X[:, b, n, :])
                own.add(last)
                hold(dve, dve_step, own.value())
                for n in range(TPB):
                    last = v.bn_aggr(meanvar[:, n, :], stats[:, n, :])
                last.then_inc(stats_ready, 1)

            def normalise(h, b):
                dve.wait_ge(std_ready, h + 1)
                own.add(v.reciprocal(rstd[:, :], std[:, :]))
                own.settle()
                if not (isinstance(h, int) and h == 0):
                    dve.wait_ge(hT_full, h)
                for n in range(TPB):
                    last = v.tensor_scalar(hn[:, n, :], X[:, b, n, :], meanvar[:, n, 0:1], rstd[:, n:n + 1],
                                           ALU.subtract, ALU.mult)
                last.then_inc(hn_ready, 1)

            def operand_rest(b, p):
                odd = p % 2
                dve.wait_ge(ghi_ready, NB * (p - 1) + b + 1)
                if p == 2:
                    last = v.tensor_tensor(flat(G_lo[odd], b), ps[:, GB, :], flat(G_hi[odd], b).bitcast(fp32),
                                           ALU.subtract)
                else:
                    for n in range(TPB):
                        last = v.scalar_tensor_tensor(
                            G_lo[odd][:, b, n, :], ps[:, GB, n * P:(n + 1) * P],
                            inv_root[:, b, 1 if p == 1 else 0, n:n + 1],
                            G_hi[odd][:, b, n, :].bitcast(fp32), ALU.mult, ALU.subtract)
                last.then_inc(g_ready, 1)

            def sum_pieces(b, after):
                if not (isinstance(b, int) and b == 0):
                    dve.wait_ge(degree_full, b)
                for u in range(UNITS):
                    dve.wait_ge(at_loaded[u % SLOTS], loaded_value(b, u))
                    half = colsum[:, u % 2 * UK:u % 2 * UK + UK, :]
                    if u < 2:
                        ins = v.tensor_copy(half, ring[:, u % SLOTS, :, :])
                    else:
                        dve.wait_ge(summed, UNITS * b + u - 1)
                        ins = v.tensor_tensor(half, half, ring[:, u % SLOTS, :, :], ALU.add)
                    ins.then_inc(summed, 1)
                    if u in after:
                        after[u]()
                dve.wait_ge(summed, UNITS * (b + 1))
                own.add(v.tensor_tensor(colsum[:, 0:2, :], colsum[:, 0:2, :], colsum[:, 2:4, :], ALU.add))
                own.settle()
                v.tensor_tensor(colsum[:, 0, :], colsum[:, 0, :], colsum[:, 1, :],
                                ALU.add).then_inc(colsum_ready, 1)

            def degrees(b):
                dve.wait_ge(degree_full, b + 1)
                if not (isinstance(b, int) and b == 0):
                    dve.wait_ge(root_ready, b)
                v.tensor_copy(degree[:, b, :], ps[:, AUX, 0:TPB])
                v.tensor_copy(deg_pair[:, 0, :], ps[:, AUX, 0:TPB])
                v.tensor_scalar(deg_pair[:, 1, :], ps[:, AUX, 0:TPB], 1.0, None, ALU.add).then_inc(pair_ready, 1)

            def inverse_roots(b):
                dve.wait_ge(root_ready, b + 1)
                v.reciprocal(inv_root[:, b, :, :], deg_root[:, :, :]).then_inc(inv_ready, 1)

            def add_rows(p, b):
                dve.wait_ge(nat_full, NB * p + b + 1)
                own.add(v.tensor_tensor(rows_of(X, b), rows_of(X, b), ps[:, TB, :], ALU.add))
                hold(dve, dve_step, own.value())

            def l1_rows(b):
                q = NB + b
                dve.wait_ge(nat_full, q + 1)
                sums = nat[:, :, :].rearrange("p t f -> p (t f)")
                own.add(v.tensor_tensor(sums, rows_of(G_lo[1], b).bitcast(fp32), ps[:, TB, :], ALU.add))
                own.settle()
                own.add(v.tensor_tensor(sums, sums, rows_of(G_hi[1], b).bitcast(fp32), ALU.add))
                own.settle()
                for n in range(TPB):
                    last = v.scalar_tensor_tensor(nat[:, n, :], nat[:, n, :], inv_root[:, b, 1, n:n + 1],
                                                  w(ROW_L1), ALU.mult, ALU.add)
                last.then_inc(v_ready, 1)

            def square_floor(b):
                dve.wait_ge(ss_ready, b + 1)
                v.tensor_scalar(ssum[:, :], ssum[:, :], 1e-24, None, ALU.max).then_inc(ssmax_ready, 1)

            def add_unit_rows(b):
                dve.wait_ge(norm_ready, b + 1)
                own.add(v.reciprocal(rstd[:, :], norm[:, :]))
                own.settle()
                for n in range(TPB):
                    last = v.scalar_tensor_tensor(X[:, b, n, :], nat[:, n, :], rstd[:, n:n + 1], X[:, b, n, :],
                                                  ALU.mult, ALU.add)
                own.add(last)
                hold(dve, dve_step, own.value())

            def reset(b):
                dve.wait_ge(rz_ready, b + 1)
                own.add(v.scalar_tensor_tensor(cand, ps[:, AUX + 3, :], col(C_HN), gate_r[:, :],
                                               ALU.add, ALU.mult))
                own.settle()
                v.tensor_tensor(cand, cand, ps[:, AUX + 2, :], ALU.add).then_inc(t_ready, 1)

            def update(b):
                dve.wait_ge(n_ready, b + 1)
                own.add(v.tensor_tensor(cand, HT[:, b, :], hTs[:, :], ALU.subtract))
                own.settle()
                own.add(v.tensor_tensor(cand, cand, gate_z, ALU.mult))
                own.settle()
                v.tensor_tensor(cand, cand, hTs[:, :], ALU.add).then_inc(u_ready, 1)

            def lap_rows(b):
                dve.wait_ge(nat_full, 3 * NB + b + 1)
                for n in range(TPB):
                    last = v.scalar_tensor_tensor(nat[:, n, :], ps[:, TB, n * P:(n + 1) * P],
                                                  inv_root[:, b, 0, n:n + 1], w(ROW_LAP1), ALU.mult, ALU.add)
                own.add(last)
                own.settle()
                z = nat[:, :, :].rearrange("p t f -> p (t f)")
                v.scalar_tensor_tensor(z, z, 0.1, z, ALU.mult, ALU.max).then_inc(z_ready, 1)

            def square_parts(b):
                dve.wait_ge(sqrow_full, b + 1)
                row = ps[0:3, GB, :]
                own.add(v.tensor_copy(part_hi[:, :], row))
                own.settle()
                own.add(v.tensor_tensor(rest[:, :], row, part_hi[:, :], ALU.subtract))
                own.settle()
                own.add(v.tensor_copy(part_mid[:, :], rest[:, :]))
                own.settle()
                own.add(v.tensor_tensor(rest[:, :], rest[:, :], part_mid[:, :], ALU.subtract))
                own.add(v.tensor_scalar(mixed[:, :], part_hi[:, :], pack[0:3, 0:1], None, ALU.mult))
                own.settle()
                own.add(v.scalar_tensor_tensor(mixed[:, :], part_mid[:, :], pack[0:3, 1:2], mixed[:, :],
                                               ALU.mult, ALU.add))
                own.settle()
                v.scalar_tensor_tensor(sq_aug[:, b, :], rest[:, :], pack[0:3, 2:3], mixed[:, :],
                                       ALU.mult, ALU.add).then_inc(aug_ready, 1)

            def steps(p, b):
                h = NB * (p + 1) + b
                tail = (lambda: normalise(h, b), lambda: operand_rest(b, p + 1))
                return ((lambda: degrees(b), lambda: (inverse_roots(b), add_rows(0, b), statistics(h, b)), *tail),
                        (lambda: l1_rows(b), lambda: square_floor(b),
                         lambda: (add_unit_rows(b), statistics(h, b)), *tail),
                        (lambda: reset(b), lambda: update(b),
                         lambda: (add_rows(2, b), statistics(h, b)), *tail),
                        (lambda: lap_rows(b), lambda: square_parts(b)),
                        (lambda: weigh(b, 0), lambda: weigh(b, 1), lambda: weigh(b, 2), lambda: weigh(b, 3),
                         lambda: last_rows(b)))[p]

            def over(at_units, p, b):
                return dict(zip(at_units, steps(p, b)))

            def lower_block(q, after):
                for u in range(UNITS):
                    if not whole(u):
                        dve.wait_ge(upper_ready, split_count(q, u))
                        v.tensor_tensor(A_lo[:, rank(u) % STAGED, :, :], ring[:, u % SLOTS, :, :],
                                        A_hi[:, rank(u) % STAGED, :, :].bitcast(fp32),
                                        ALU.subtract).then_inc(lower_ready, 1)
                    if u in after:
                        after[u]()

            def whole_rows(p, j):
                m, kk = (4 * j + 3) // 2, (4 * j + 3) % 2 * UK
                dve.wait_ge(used, UNITS * NB * p)
                dve.wait_ge(g_ready, NB * p + m + 1)
                v.tensor_tensor(G_whole[:, j, :, :], G_hi[p % 2][:, m, kk:kk + UK, :].bitcast(fp32),
                                G_lo[p % 2][:, m, kk:kk + UK, :].bitcast(fp32), ALU.add).then_inc(whole_ready, 1)

            def with_whole_rows(p, after):
                both = dict(after)
                for j, u in enumerate(WHOLE_AT[p]):
                    first = after.get(u, lambda: None)
                    both[u] = lambda j=j, first=first: (first(), whole_rows(p, j))
                return both

            def counted(loop, bodies, expected):
                start = own.value()
                with loop as b:
                    own.turn(start + (b - 1) * expected)
                    bodies(b)
                    assert own.n == expected, own.n
                return start

            dve.wait_ge(pack_loaded, 16)
            v.tensor_tensor(gate_bias[:, :], pack[:, 16 * P + C_IR:16 * P + C_IR + 2],
                            pack[:, 16 * P + C_HR:16 * P + C_HR + 2], ALU.add).then_inc(bias_ready, 1)
            for b in range(NB):
                dve.wait_ge(x_loaded[b], 16)
                statistics(b, b)
                normalise(b, b)

            sum_pieces(0, {})
            start = counted(dve.Fori(1, NB), lambda b: sum_pieces(b, over(DVE_FIRST, 0, b - 1)), DVE_STEPS[0])
            own.turn(start + (NB - 1) * DVE_STEPS[0])
            for p in range(1, 4):
                lower_block(NB * p, with_whole_rows(p, over(DVE_TURN[p - 1], p - 1, NB - 1)))
                start = counted(dve.Fori(1, NB),
                                lambda b: lower_block(NB * p + b, over(DVE_AT[p], p, b - 1)), DVE_STEPS[p])
                own.turn(start + (NB - 1) * DVE_STEPS[p])
            for step in steps(3, NB - 1):
                step()

            dve.wait_ge(z2_ready, NB)
            v.tensor_scalar(neg_sq[:, :], neg_sq[:, :], -1.0, None, ALU.mult).then_inc(negsq_ready, 1)

            def scan(t, odd):
                dve.wait_ge(half_out, 2 * t + 2)
                row = scores[odd][:, :]
                own.add(v.max(best[:, t, :], row))
                own.settle()
                v.max_index(best_at[:, t, :], best[:, t, :], row).then_inc(scanned, 1)

            for t in range(NT):
                scan(t, t % 2)

            dve.wait_ge(scanned, NT)
            v.tensor_scalar(simil[:, :, :], best[:, :, 0:TOPK], 0.0, None, ALU.min).then_inc(clamp_ready, 1)
            dve.wait_ge(simil_ready, 1)
            own.add(v.reduce_sum(deg2[:, :], simil[:, :, :], axis=mybir.AxisListType.X))
            own.settle()
            v.tensor_tensor(deg2[:, :], deg2[:, :], degree[:, :, :].rearrange("p b t -> p (b t)"),
                            ALU.add).then_inc(deg2_ready, 1)
            dve.wait_ge(root2_ready, 1)
            own.add(v.reciprocal(d2inv[:, :], root2[:, :]))
            own.settle()
            for b in range(NB):
                for n in range(TPB):
                    last = v.tensor_scalar(G_last[:, b, n, :], G_last[:, b, n, :],
                                           d2inv[:, b * TPB + n:b * TPB + n + 1], None, ALU.mult)
                last.then_inc(last_ready, 1)
            for b in range(NB):
                dve.wait_ge(lasthi_ready, b + 1)
                v.tensor_tensor(flat(G_lo[1], b), flat(G_last, b), flat(G_hi[1], b).bitcast(fp32),
                                ALU.subtract).then_inc(lastlo_ready, 1)

            def weigh(b, k):
                dve.wait_ge(gathered[k], 16 * TOPK * (b + 1))
                slot, dst, t = landing[:, k, :, :], near[:, b, k, :], b * TPB + k
                own.add(v.tensor_scalar(dst, slot[:, 0, :], simil[:, t, 0:1], None, ALU.mult))
                for r in range(1, TOPK):
                    own.settle()
                    ins = v.scalar_tensor_tensor(dst, slot[:, r, :], simil[:, t, r:r + 1], dst,
                                                 ALU.mult, ALU.add)
                    if r < TOPK - 1:
                        own.add(ins)
                ins.then_inc(weighted, 1)

            def last_rows(b):
                dve.wait_ge(weighted, TPB * b + TPB)
                dve.wait_ge(nat_full, 4 * NB + b + 1)
                own.add(v.tensor_tensor(nat[:, :, :].rearrange("p t f -> p (t f)"), rows_of(near, b),
                                        ps[:, TB, :], ALU.add))
                own.settle()
                for n in range(TPB):
                    last = v.scalar_tensor_tensor(nat[:, n, :], nat[:, n, :],
                                                  d2inv[:, bass.ds(b * TPB + n, 1)],
                                                  w(ROW_LAP2), ALU.mult, ALU.add)
                own.add(last)
                own.settle()
                v.tensor_tensor(rows_of(X, b), rows_of(X, b), nat[:, :, :].rearrange("p t f -> p (t f)"),
                                ALU.add).then_inc(x_final, 1)

            lower_block(4 * NB, {})
            start = counted(dve.Fori(1, NB),
                            lambda b: lower_block(4 * NB + b, over(DVE_AT[4], 4, b - 1)), DVE_STEPS[4])
            own.turn(start + (NB - 1) * DVE_STEPS[4])
            for step in steps(4, NB - 1):
                step()

        @block.gpsimd
        def _(pool):
            g = nc.gpsimd
            g.memset(ones3[:, :], 1.0)
            g.memset(halves[:, :], -0.5)
            g.memset(ones[:, :], 1.0)
            g.memset(eps_ln[:, :], 1e-5)
            g.memset(eps_d2[:, :], 1e-10).then_inc(consts_set, 1)

            pool.wait_ge(last_ready, NB)
            pool.dma_start(scaled_rows.rearrange("(b t p) f -> p (b t) f", t=TPB, p=P),
                           G_last.rearrange("p b t f -> p (b t) f")).then_inc(rows_stored, 16)
            pool.wait_ge(rows_stored, 16)

            def gather(t, k):
                if not (isinstance(t, int) and t < GSLOTS):
                    pool.wait_ge(weighted, t - GSLOTS + 1)
                g.tensor_copy(picks[:, k, :], best_at[:, t, 0:TOPK]).then_inc(picks_ready, 1)
                hold(pool, picks_ready, t + 1)
                for r in range(TOPK):
                    pool.indirect_dma_start(
                        out=landing[:, k, r, :], out_offset=None, in_=scaled_rows,
                        in_offset=bass.IndirectOffsetOnAxis(ap=picks[:, k, r:r + 1], axis=0),
                    ).then_inc(gathered[k], 16)

            for k in range(GSLOTS):
                gather(k, k)
            with pool.Fori(1, NT // GSLOTS) as turn:
                for k in range(GSLOTS):
                    gather(GSLOTS * turn + k, k)


PE_FIRST, DVE_FIRST = (1, 7, 11), (1, 3, 5, 11)
PE_AT = {1: (0, 10, 11), 2: (0, 6, 10, 11), 3: (0, 6, 9), 4: (5,)}
ACT_AT = {1: (4, 7, 8, 10, 13, 15), 2: (0, 5, 6, 11, 13, 14), 3: (2, 6, 10), 4: (4, 15)}
DVE_AT = {1: (4, 6, 8, 11, 15), 2: (5, 7, 9, 11, 14), 3: (3, 14), 4: (0, 2, 6, 7, 12)}
PE_TURN = {0: (0, 9, 10), 1: (0, 10, 11), 2: (0, 5, 10, 11)}
ACT_TURN = {0: (1, 7, 10, 12, 13), 1: (4, 7, 8, 11, 13, 15), 2: (0, 5, 6, 11, 13, 14)}
DVE_TURN = {0: (3, 6, 9, 13), 1: (4, 5, 8, 11, 15), 2: (5, 6, 8, 11, 14)}
WHOLE_AT = {1: (2, 3, 10, 15), 2: (2, 4, 11, 15), 3: (1, 4, 11, 15)}
DVE_STEPS = (4, 6, 6, 7, 14)


def kernel(**inputs):
    import numpy as np
    import concourse.bacc as bacc
    from concourse.bass_utils import run_bass_kernel_spmd

    fp32 = mybir.dt.float32
    get = lambda n: np.asarray(inputs[n])
    x = np.ascontiguousarray(get("x").reshape(NB, TPB, P, P).transpose(2, 0, 1, 3))
    at = np.ascontiguousarray(get("adj").reshape(NB, BLK, UNITS, UK, P).transpose(0, 2, 4, 3, 1))
    w0, w1, wm = get("L0_gnn_W"), get("L1_gnn_W"), get("L2_gnn_W_msg")
    wi, wh = get("L2_gnn_W_ih"), get("L2_gnn_W_hh")
    bi, bh = get("L2_gnn_b_ih").reshape(3, P), get("L2_gnn_b_hh").reshape(3, P)
    mats = [np.eye(P, dtype=np.float32), w0[:, :P].T, w0[:, P:].T, w1.T, wm.T]
    mats += [wi[g * P:(g + 1) * P].T for g in range(3)] + [wh[g * P:(g + 1) * P].T for g in range(3)]
    mats += [get("L3_gnn_W1"), get("L3_gnn_W2")]
    mats += [np.broadcast_to(get(n), (P, P)) for n in ("L1_gnn_b", "L3_gnn_b1", "L3_gnn_b2")]
    cols = [get("L0_gnn_b"), get("L2_gnn_b_msg"), bi[0], bi[1], bi[2], bh[0], bh[1], bh[2]]
    pack = np.ascontiguousarray(np.concatenate(mats + [c.reshape(P, 1) for c in cols], axis=1))

    nc = bacc.Bacc("TRN2", target_bir_lowering=False, num_devices=1, dynamic_dma_scratch_size=8192)
    arrays = {"x_rows": x, "adj_t": at, "packed": pack}
    aps = [nc.dram_tensor(n, a.shape, fp32, kind="ExternalInput").ap() for n, a in arrays.items()]
    scaled_rows = nc.dram_tensor("scaled_rows", (N, P), fp32, kind="Internal").ap()
    out = nc.dram_tensor("out_rows", (NB, P, TPB, P), fp32, kind="ExternalOutput").ap()
    gnn_stack(nc, *aps, scaled_rows, out)
    r = run_bass_kernel_spmd(nc, [arrays], core_ids=[0])
    got = r.results[0]["out_rows"]
    return np.ascontiguousarray(got.transpose(0, 2, 1, 3)).reshape(N, P)
```

```python
import concourse.bass as bass
from concourse import mybir
from contextlib import ExitStack

P = 128
N = 4096
BLK = 512
TPB = BLK // P
NB = N // BLK
NT = N // P
LAYERS = 5
UK = 2
UNITS = N // P // UK
SLOTS = 8
STAGED = 4
TOPK = 4
GSLOTS = 4

(IDENT, W_SELF, W_NEIGH, W_L1, W_MSG, W_IR, W_IZ, W_IN, W_HR, W_HZ, W_HN, W_LAP1, W_LAP2,
 ROW_L1, ROW_LAP1, ROW_LAP2) = range(16)
(C_L0, C_MSG, C_IR, C_IZ, C_IN, C_HR, C_HZ, C_HN) = range(8)
PACK = 16 * P + 8


class Steps:

    def __init__(self, eng, sem):
        self.eng, self.sem, self.base, self.n = eng, sem, 0, 0

    def add(self, ins):
        ins.then_inc(self.sem, 1)
        self.n += 1

    def value(self):
        return self.base + self.n

    def settle(self):
        self.eng.wait_ge(self.sem, self.value())

    def turn(self, base):
        self.base, self.n = base, 0


def behind_units(at_units, steps):
    groups = {}
    for u, step in zip(at_units, steps):
        groups.setdefault(u, []).append(step)
    return {u: lambda group=group: [step() for step in group] for u, group in groups.items()}


def loaded_value(q, u):
    return 16 * (UNITS // SLOTS * q + u // SLOTS + 1)


WHOLE = {1: (3, 7, 11, 15), 2: (3, 7, 11, 15), 3: (3, 7, 11, 15), 4: (7, 15)}
WHOLE_BESIDE_SCANS = (*range(10), 14, 15)


SPLIT_FIRST = (7, 10, 14)


def whole_units(p, b):
    at_start = isinstance(b, int) and b == 0
    if p == 0:
        return [u for u in range(UNITS) if at_start or u not in SPLIT_FIRST]
    return WHOLE_BESIDE_SCANS if p == 4 and at_start else WHOLE[p]


def split_units(p, b):
    return [u for u in range(UNITS) if u not in whole_units(p, b)]


def staged_slot(p, b, u):
    return split_units(p, b).index(u) % STAGED


def split_count(p, b, u):
    ahead = sum(len(split_units(a, c)) for a in range(p) for c in range(NB))
    if not isinstance(b, int) or b > 0:
        ahead = len(split_units(p, 0)) + len(split_units(p, 1)) * (b - 1) + ahead
    return ahead + split_units(p, b).index(u) + 1


def before(p, b):
    return (p, b - 1) if not isinstance(b, int) or b > 0 else (p - 1, NB - 1)


def used_before(p, b, u):
    slot, same = staged_slot(p, b, u), [x for x in split_units(p, b) if x < u]
    if not any(staged_slot(p, b, x) == slot for x in same):
        p, b = before(p, b)
        same = split_units(p, b)
    held = [x for x in same if staged_slot(p, b, x) == slot]
    return UNITS * (NB * p + b) + held[-1] + 1 if held else None


def whole_count(p, u):
    return sum(len(WHOLE[a]) for a in range(1, p)) + WHOLE[p].index(u) + 1


def gnn_stack(nc, x_in, at_in, pack_in, scaled_rows, out):
    fp32, bf16, u32 = mybir.dt.float32, mybir.dt.bfloat16, mybir.dt.uint32
    ALU, ACT = mybir.AluOpType, mybir.ActivationFunctionType

    ctx = ExitStack()
    with ctx:
        def sb(name, shape, dt=fp32):
            return ctx.enter_context(nc.sbuf_tensor(name, shape, dt))

        def sem(name):
            return ctx.enter_context(nc.semaphore(name))

        r32 = mybir.dt.float32r
        place = [(nc.sbuf_base + 31) // 32 * 32]

        def at(name, shape, dt, offset):
            return nc.alloc_sbuf_tensor_at(name, shape, dt, offset=offset)

        def take(name, kib):
            place[0] += kib * 1024
            ctx.enter_context(nc.sbuf_tensor(name, [P, kib * 256], fp32))
            return place[0] - kib * 1024

        even, odd_at, last_at = take("area_even", 32), take("area_odd", 32), take("area_last", 16)
        G_hi = [at("G_even_hi", [P, NB, TPB, P], r32, even), at("G_odd_hi", [P, NB, TPB, P], r32, odd_at)]
        G_lo = [at("G_even_lo", [P, NB, TPB, P], r32, even + 16384),
                at("G_odd_lo", [P, NB, TPB, P], r32, odd_at + 16384)]
        G_first = at("G_first", [P, NB, TPB, P], fp32, even)
        scores = [at(f"scores{n}", [P, N], fp32, even + 16384 * n) for n in range(2)]
        near = at("near", [P, TPB, P], fp32, even)
        landing = at("landing", [P, GSLOTS, TOPK, P], fp32, even + 16384)
        X = sb("X", [P, NB, TPB, P])
        G_last = at("G_last", [P, NB, TPB, P], fp32, last_at)
        G_first_hi = at("G_first_hi", [P, len(SPLIT_FIRST), UK, P], r32, last_at)
        G_first_lo = at("G_first_lo", [P, len(SPLIT_FIRST), UK, P], r32, last_at + 8192)
        HT = sb("HT", [P, NB, BLK])
        ring = sb("ring", [P, SLOTS, UK, BLK])
        A_hi = sb("A_hi", [P, STAGED, UK, BLK], r32)
        A_lo = sb("A_lo", [P, STAGED, UK, BLK], r32)
        G_whole = sb("G_whole", [P, 4, UK, P])
        pack = sb("pack", [P, PACK])
        colsum = sb("colsum", [P, TPB, BLK])
        rows_T = sb("rows_T", [P, BLK])
        gate_z = colsum[:, 2, :]
        cand = colsum[:, 3, :]
        nat = sb("nat", [P, TPB, P])
        folded = nat[:, :, :].rearrange("p t f -> p (t f)")
        hn = sb("hn", [P, TPB, P])
        gate_r = hn[:, :, :].rearrange("p t f -> p (t f)")
        hTs = sb("hTs", [P, BLK])
        stats = sb("stats", [P, 2, TPB, 6])
        meanvar = sb("meanvar", [P, 2, TPB, 2])
        std = sb("std", [P, 2, TPB])
        rstd = sb("rstd", [P, TPB])
        degree = sb("degree", [P, NB, TPB])
        deg_pair = sb("deg_pair", [P, 2, TPB])
        deg_root = sb("deg_root", [P, 2, TPB])
        inv_root = sb("inv_root", [P, NB, 2, TPB])
        ssum = sb("ssum", [P, TPB])
        norm = sb("norm", [P, TPB])
        neg_sq = sb("neg_sq", [P, NT])
        sq_aug = colsum[0:3, :, :].bitcast(bf16).rearrange("p t (b n) -> p (t b) n", n=BLK)
        part_hi = sb("part_hi", [3, BLK], bf16)
        part_mid = sb("part_mid", [3, BLK], bf16)
        rest = sb("rest", [3, BLK])
        mixed = sb("mixed", [3, BLK])
        ones3 = sb("ones3", [3, P], bf16)
        halves = sb("halves", [P, 3])
        ones = sb("ones", [P, 1])
        eps_ln = sb("eps_ln", [P, 1])
        eps_d2 = sb("eps_d2", [P, 1])
        gate_bias = sb("gate_bias", [P, 2])
        best = rows_T[:, 0:NT * 8].rearrange("p (t e) -> p t e", e=8)
        best_at = sb("best_at", [P, NT, 8], u32)
        picks = sb("picks", [P, GSLOTS, TOPK], u32)
        simil = sb("simil", [P, NT, TOPK])
        deg2 = sb("deg2", [P, NT])
        root2 = sb("root2", [P, NT])
        d2inv = sb("d2inv", [P, NT])
        ps = ctx.enter_context(nc.psum_tensor("ps", [P, 8, BLK], fp32))
        TB, GB, AUX = 2, 3, 4

        w = lambda i: pack[:, i * P:(i + 1) * P]
        col = lambda i: pack[:, 16 * P + i:16 * P + i + 1]
        ident = w(IDENT)
        flat = lambda t, b: t[:, b, :, :].rearrange("p t f -> p (t f)")

        pack_loaded, rest_loaded, consts_set = sem("pack_loaded"), sem("rest_loaded"), sem("consts_set")
        x_loaded = [sem(f"x_loaded{b}") for b in range(NB)]
        at_loaded = [sem(f"at_loaded{s}") for s in range(SLOTS)]
        used, summed = sem("used"), sem("summed")
        upper_ready, lower_ready = sem("upper_ready"), sem("lower_ready")
        whole_ready = sem("whole_ready")
        firsthi_ready, firstlo_ready = sem("firsthi_ready"), sem("firstlo_ready")
        rowsT_ready, nat_full = sem("rowsT_ready"), sem("nat_full")
        stats_ready, std_ready, hn_ready = sem("stats_ready"), sem("std_ready"), sem("hn_ready")
        hT_full, hTs_ready, g_full, g_ready = sem("hT_full"), sem("hTs_ready"), sem("g_full"), sem("g_ready")
        ghi_ready = sem("ghi_ready")
        raw_full, raw_ready = sem("raw_full"), sem("raw_ready")
        colsum_ready, degree_full = sem("colsum_ready"), sem("degree_full")
        pair_ready, root_ready, inv_ready = sem("pair_ready"), sem("root_ready"), sem("inv_ready")
        v_ready, ss_ready, ssmax_ready, norm_ready = sem("v_ready"), sem("ss_ready"), sem("ssmax_ready"), sem("norm_ready")
        gates_full, rz_ready, t_ready, n_ready, u_ready = (
            sem("gates_full"), sem("rz_ready"), sem("t_ready"), sem("n_ready"), sem("u_ready"))
        z_ready, zT_full, z2_ready, sqrow_full, aug_ready = (
            sem("z_ready"), sem("zT_full"), sem("z2_ready"), sem("sqrow_full"), sem("aug_ready"))
        ztile_ready, half_full, half_out, scanned = sem("ztile_ready"), sem("half_full"), sem("half_out"), sem("scanned")
        clamp_ready, dist_ready, simil_ready, deg2_ready, root2_ready = (
            sem("clamp_ready"), sem("dist_ready"), sem("simil_ready"), sem("deg2_ready"), sem("root2_ready"))
        last_ready, lasthi_ready, lastlo_ready = sem("last_ready"), sem("lasthi_ready"), sem("lastlo_ready")
        zss_ready, negsq_ready = sem("zss_ready"), sem("negsq_ready")
        d2_ready, scaled_ready = sem("d2_ready"), sem("scaled_ready")
        rows_stored = sem("rows_stored")
        gathered = [sem(f"gathered{s}") for s in range(GSLOTS)]
        picks_ready = sem("picks_ready")
        weighted, x_final, out_stored = sem("weighted"), sem("x_final"), sem("out_stored")
        bias_ready, dve_step = sem("bias_ready"), sem("dve_step")

        SPARES = 8
        spare = sb("spare", [P, 3 * SPARES])
        holds = [0]

        def hold(eng, semaphore, value):
            eng.wait_ge(semaphore, value)
            if isinstance(value, int):
                return
            holds[0] += 1
            at = lambda e: spare[:, e * SPARES + holds[0] % SPARES:e * SPARES + holds[0] % SPARES + 1]
            if eng is nc.vector:
                nc.vector.memset(at(0), 0.0)
            elif eng is nc.scalar:
                nc.scalar.activation(at(1), ones[:, :], ACT.Copy)
            else:
                nc.gpsimd.tensor_tensor(at(2), ones[:, :], ones[:, :], ALU.add)

        pair_bank = lambda c: (c + 4) % 8
        acc_bank = lambda p, b: b % 2 + (4 if p == 4 else 0)
        first_hn, first_hTs = (hn, nat), (hTs, rows_T)
        first_hT, first_G = (TB, AUX), (GB, AUX + 1)

        block = ctx.enter_context(nc.Block())

        @block.sync
        def _(sp):
            def load_x(b):
                sp.dma_start(X[:, b, :, :], x_in[:, b, :, :]).then_inc(x_loaded[b], 16)

            def load_unit(q, u):
                sp.dma_start(ring[:, u % SLOTS, :, :], at_in[q, u, :, :, :]).then_inc(at_loaded[u % SLOTS], 16)

            def load_first(b, u_from=0):
                for u in range(u_from, UNITS):
                    last = UNITS * b + u - SLOTS
                    sp.wait_ge(used, last + 1)
                    sp.wait_ge(summed, last + 1)
                    load_unit(b, u)

            def load_block(p, b):
                for u in range(UNITS):
                    (lp, lb), lu = ((p, b), u - SLOTS) if u >= SLOTS else (before(p, b), u + UNITS - SLOTS)
                    held = UNITS * (NB * lp + lb) + lu + 1
                    if lp == 0:
                        sp.wait_ge(used, held)
                        sp.wait_ge(summed, held)
                    elif lu in whole_units(lp, lb):
                        sp.wait_ge(used, held)
                    else:
                        sp.wait_ge(lower_ready, split_count(lp, lb, lu))
                    load_unit(b, u)

            load_x(0)
            sp.dma_start(pack[:, 0:3 * P], pack_in[:, 0:3 * P]).then_inc(pack_loaded, 16)
            load_x(1)
            for u in range(SLOTS):
                load_unit(0, u)
                if u + 2 < NB:
                    load_x(u + 2)
            sp.dma_start(pack[:, 3 * P:PACK], pack_in[:, 3 * P:PACK]).then_inc(rest_loaded, 16)
            load_first(0, SLOTS)
            with sp.Fori(1, NB) as b:
                load_first(b)
            for p in range(1, LAYERS - 1):
                load_block(p, 0)
                with sp.Fori(1, NB) as b:
                    load_block(p, b)

            def send(b):
                sp.wait_ge(x_final, b + 1)
                sp.dma_start(out[b, :, :, :], X[:, b, :, :]).then_inc(out_stored, 16)

            load_block(4, 0)
            load_block(4, 1)
            with sp.Fori(2, NB) as b:
                load_block(4, b)
                send(b - 2)
            send(NB - 2)
            send(NB - 1)
            sp.wait_ge(out_stored, 16 * NB)

        @block.tensor
        def _(pe):
            mm = nc.tensor.matmul

            def first_block(b, after):
                acc = ps[:, acc_bank(0, b), :]
                if isinstance(b, int):
                    pe.wait_ge(hTs_ready, 1)
                else:
                    pe.wait_ge(rowsT_ready, b - 1)
                mm(acc, w(W_SELF), HT[:, b, :], start=True, stop=False)
                for u in range(UNITS):
                    if isinstance(b, int) and u % 2 == 0:
                        pe.wait_ge(g_ready, u // 2 + 1)
                    if u in split_units(0, b):
                        i, slot = SPLIT_FIRST.index(u), staged_slot(0, b, u)
                        pe.wait_ge(firstlo_ready, len(SPLIT_FIRST))
                        pe.wait_ge(lower_ready, split_count(0, b, u))
                        for k in range(UK):
                            mm(acc, G_first_hi[:, i, k, :], A_hi[:, slot, k, :], start=False, stop=False)
                            mm(acc, G_first_hi[:, i, k, :], A_lo[:, slot, k, :], start=False, stop=False)
                            last = mm(acc, G_first_lo[:, i, k, :], A_hi[:, slot, k, :], start=False, stop=False)
                        last.then_inc(used, 1)
                        if u in after:
                            after[u]()
                        continue
                    pe.wait_ge(at_loaded[u % SLOTS], loaded_value(b, u))
                    for k in range(UK):
                        last = mm(acc, G_first[:, u // 2, u % 2 * UK + k, :], ring[:, u % SLOTS, k, :],
                                  start=False, stop=(u == UNITS - 1 and k == UK - 1))
                    last.then_inc(used, 1)
                    if u in after:
                        after[u]()

            def split_block(p, b, after):
                q = NB * p + b
                odd = 1 if p == 4 else p % 2
                acc = ps[:, acc_bank(p, b), :]
                pe.wait_ge(rowsT_ready, q - 1)
                for u in range(UNITS):
                    m, whole = u // 2, u in whole_units(p, b)
                    if isinstance(b, int):
                        if p == 4 and b == 0:
                            pe.wait_ge(last_ready if whole else lastlo_ready, m + 1)
                        elif p == 4:
                            pe.wait_ge(lastlo_ready, NB)
                        elif whole:
                            pe.wait_ge(whole_ready, whole_count(p, u))
                        else:
                            pe.wait_ge(g_ready, NB * p + m + 1)
                    if whole:
                        pe.wait_ge(at_loaded[u % SLOTS], loaded_value(q, u))
                    else:
                        pe.wait_ge(lower_ready, split_count(p, b, u))
                    for k in range(UK):
                        kk = u % 2 * UK + k
                        begin, end = u == 0 and k == 0, u == UNITS - 1 and k == UK - 1
                        if whole:
                            G = G_last[:, m, kk, :] if p == 4 else G_whole[:, WHOLE[p].index(u), k, :]
                            last = mm(acc, G, ring[:, u % SLOTS, k, :], start=begin, stop=end)
                        else:
                            slot = staged_slot(p, b, u)
                            hi, lo = A_hi[:, slot, k, :], A_lo[:, slot, k, :]
                            mm(acc, G_hi[odd][:, m, kk, :], hi, start=begin, stop=False)
                            mm(acc, G_hi[odd][:, m, kk, :], lo, start=False, stop=False)
                            last = mm(acc, G_lo[odd][:, m, kk, :], hi, start=False, stop=end)
                    last.then_inc(used, 1)
                    if u in after:
                        after[u]()

            def to_natural(p, b):
                q = NB * p + b
                if p == 2:
                    pe.wait_ge(u_ready, b + 1)
                    src = cand
                else:
                    pe.wait_ge(rowsT_ready, q + 1)
                    src = rows_T
                if p == 3 and not (isinstance(b, int) and b == 0):
                    pe.wait_ge(z2_ready, b)
                elif p == 4:
                    if not (isinstance(b, int) and b == 0):
                        pe.wait_ge(x_final, b)
                else:
                    pe.wait_ge(hTs_ready, q + NB)
                for n in range(TPB):
                    last = nc.tensor.transpose(ps[:, TB, n * P:(n + 1) * P], src[:, n * P:(n + 1) * P], ident)
                last.then_inc(nat_full, 1)

            def h_transposes(h):
                pe.wait_ge(hn_ready, h + 1)
                pe.wait_ge(hTs_ready, h)
                for n in range(TPB):
                    last = nc.tensor.transpose(ps[:, TB, n * P:(n + 1) * P], hn[:, n, :], ident)
                last.then_inc(hT_full, 1)

            def first_transposes(b):
                pe.wait_ge(hn_ready, b + 1)
                if b >= 2:
                    pe.wait_ge(hTs_ready, b - 1)
                for n in range(TPB):
                    last = nc.tensor.transpose(ps[:, first_hT[b % 2], n * P:(n + 1) * P],
                                               first_hn[b % 2][:, n, :], ident)
                last.then_inc(hT_full, 1)

            def first_operand(b):
                pe.wait_ge(hTs_ready, b + 1)
                if b >= 2:
                    pe.wait_ge(g_ready, b - 1)
                for n in range(TPB):
                    last = mm(ps[:, first_G[b % 2], n * P:(n + 1) * P],
                              first_hTs[b % 2][:, n * P:(n + 1) * P], w(W_NEIGH), start=True, stop=True)
                last.then_inc(g_full, 1)

            def operand(h, weight, raw=None):
                pe.wait_ge(hTs_ready, h + 1)
                pe.wait_ge(g_ready, h)
                for n in range(TPB):
                    last = mm(ps[:, GB, n * P:(n + 1) * P], hTs[:, n * P:(n + 1) * P], w(weight),
                              start=True, stop=True)
                last.then_inc(g_full, 1)
                if raw is not None:
                    for n in range(TPB):
                        last = mm(ps[:, AUX, n * P:(n + 1) * P], hTs[:, n * P:(n + 1) * P], w(raw),
                                  start=True, stop=True)
                    last.then_inc(raw_full, 1)

            def degree_sums(b):
                pe.wait_ge(colsum_ready, b + 1)
                if not (isinstance(b, int) and b == 0):
                    pe.wait_ge(pair_ready, b)
                for n in range(TPB):
                    last = mm(ps[:, AUX, n:n + 1], folded[:, n * P:(n + 1) * P], ones[:, :],
                              start=True, stop=True)
                last.then_inc(degree_full, 1)

            def gates(b):
                pe.wait_ge(rowsT_ready, 2 * NB + b + 1)
                if isinstance(b, int) and b == 0:
                    pe.wait_ge(pair_ready, NB)
                else:
                    pe.wait_ge(raw_ready, b)
                for n, (wi, wh) in enumerate(((W_IR, W_HR), (W_IZ, W_HZ))):
                    mm(ps[:, AUX + n, :], w(wi), rows_T[:, :], start=True, stop=False)
                    mm(ps[:, AUX + n, :], w(wh), HT[:, b, :], start=False, stop=True)
                mm(ps[:, AUX + 2, :], w(W_IN), rows_T[:, :], start=True, stop=True)
                mm(ps[:, AUX + 3, :], w(W_HN), HT[:, b, :], start=True, stop=True).then_inc(gates_full, 1)

            def z_transposes(b):
                pe.wait_ge(z_ready, b + 1)
                for n in range(TPB):
                    last = nc.tensor.transpose(ps[:, TB, n * P:(n + 1) * P], nat[:, n, :], ident)
                last.then_inc(zT_full, 1)

            def square_row(b):
                pe.wait_ge(z2_ready, b + 1)
                if isinstance(b, int) and b == 0:
                    pe.wait_ge(g_ready, 4 * NB)
                else:
                    pe.wait_ge(aug_ready, b)
                mm(ps[0:3, GB, :], halves[:, :], hTs[:, :], start=True, stop=True).then_inc(sqrow_full, 1)

            def steps(p, b):
                h = NB * (p + 1) + b
                natural = lambda: to_natural(p, b)
                layernormed = lambda: h_transposes(h)
                return ((lambda: (degree_sums(b), natural()), layernormed, lambda: operand(h, W_L1)),
                        (natural, layernormed, lambda: operand(h, W_MSG)),
                        (lambda: gates(b), natural, layernormed, lambda: operand(h, W_LAP1, W_LAP2)),
                        (natural, lambda: z_transposes(b), lambda: square_row(b)),
                        (natural,))[p]

            def over(at_units, p, b):
                return behind_units(at_units, steps(p, b))

            pe.wait_ge(pack_loaded, 16)
            pe.wait_ge(consts_set, 1)
            first_transposes(0)
            first_transposes(1)
            first_operand(0)

            def next_operand(b):
                if b + 1 < NB:
                    first_transposes(b + 1)
                first_operand(b)

            first_block(0, {2 * b - 2: lambda b=b: next_operand(b) for b in range(1, NB)})
            pe.wait_ge(rest_loaded, 16)
            with pe.Fori(1, NB) as b:
                first_block(b, over(PE_FIRST, 0, b - 1))
            for p in range(1, 4):
                split_block(p, 0, over(PE_TURN[p - 1], p - 1, NB - 1))
                with pe.Fori(1, NB) as b:
                    split_block(p, b, over(PE_AT[p], p, b - 1))
            def pair_columns(c, zt):
                mm(ps[:, pair_bank(c), :], zt, HT[:, c, :], start=True, stop=False)
                return mm(ps[:, pair_bank(c), :], ones3[:, :], sq_aug[:, c, :], start=False, stop=True)

            def pair_rows(t, odd):
                pe.wait_ge(ztile_ready, t)
                for half in range(2):
                    pe.wait_ge(half_out, 2 * t + half - 1)
                    for c in range(4 * half, 4 * half + 4):
                        last = pair_columns(c, (gate_r, hTs)[odd][:, 0:P])
                    last.then_inc(half_full, 1)

            def first_pairs(columns):
                for c in columns:
                    pe.wait_ge(aug_ready, c + 1)
                    last = pair_columns(c, HT[:, 0, 0:P])
                    if c % 4 == 3:
                        last.then_inc(half_full, 1)

            natural, z_turned, squares_row = steps(3, NB - 1)
            natural()
            first_pairs((0, 1))
            z_turned()
            first_pairs((2, 3))
            squares_row()
            first_pairs((4, 5, 6, 7))
            pair_rows(1, 1)
            with pe.Fori(1, NT // 2) as pair:
                t = 2 * pair
                pair_rows(t, 0)
                pair_rows(t + 1, 1)
            pe.wait_ge(half_out, 2 * NT - 1)

            split_block(4, 0, {})
            split_block(4, 1, over(PE_TURN[4], 4, 0))
            with pe.Fori(2, NB) as b:
                split_block(4, b, over(PE_AT[4], 4, b - 1))
            for step in steps(4, NB - 1):
                step()

        @block.scalar
        def _(act):
            def f(out_ap, in_ap, func, **k):
                return nc.scalar.activation(out_ap, in_ap, func, **k)

            def copy_out(p, b):
                q = NB * p + b
                act.wait_ge(used, UNITS * (q + 1))
                if p or not isinstance(b, int):
                    act.wait_ge(nat_full, q)
                if p == 0:
                    ins = f(rows_T[:, :], ps[:, acc_bank(p, b), :], ACT.Relu, bias=col(C_L0))
                elif p == 2:
                    ins = f(rows_T[:, :], ps[:, acc_bank(p, b), :], ACT.Relu, bias=col(C_MSG))
                else:
                    ins = f(rows_T[:, :], ps[:, acc_bank(p, b), :], ACT.Copy)
                ins.then_inc(rowsT_ready, 1)

            def roots(h, odd=0):
                act.wait_ge(stats_ready, h + 1)
                f(std[:, odd, :], meanvar[:, odd, :, 1], ACT.Sqrt, bias=eps_ln[:, :]).then_inc(std_ready, 1)

            def rectify(h, b, p):
                act.wait_ge(hT_full, h + 1)
                if p in (0, 2):
                    f(HT[:, b, :], ps[:, TB, :], ACT.Relu)
                f(hTs[:, :], ps[:, TB, :], ACT.Relu).then_inc(hTs_ready, 1)

            def operand_out(h, b, p):
                act.wait_ge(g_full, h + 1)
                if p == 2:
                    last = f(flat(G_hi[0], b), ps[:, GB, :], ACT.Copy)
                else:
                    hold(act, inv_ready, b + 1)
                    for n in range(TPB):
                        last = f(G_hi[1][:, b, n, :], ps[:, GB, n * P:(n + 1) * P], ACT.Copy,
                                 scale=inv_root[:, b, 1 if p == 1 else 0, n:n + 1])
                last.then_inc(ghi_ready, 1)
                if p == 3:
                    act.wait_ge(raw_full, b + 1)
                    f(flat(G_last, b), ps[:, AUX, :], ACT.Copy).then_inc(raw_ready, 1)

            def degree_roots(b):
                act.wait_ge(pair_ready, b + 1)
                f(deg_root[:, :, :], deg_pair[:, :, :], ACT.Sqrt).then_inc(root_ready, 1)

            def squares(p, b):
                act.wait_ge(v_ready if p == 1 else z_ready, b + 1)
                for n in range(TPB):
                    last = f(gate_r[:, n * P:(n + 1) * P], nat[:, n, :], ACT.Square,
                             accum_out=ssum[:, n:n + 1] if p == 1 else neg_sq[:, bass.ds(b * TPB + n, 1)])
                last.then_inc(ss_ready if p == 1 else zss_ready, 1)

            def norms(b):
                act.wait_ge(ssmax_ready, b + 1)
                f(norm[:, :], ssum[:, :], ACT.Sqrt).then_inc(norm_ready, 1)

            def sigmoids(b):
                act.wait_ge(gates_full, b + 1)
                act.wait_ge(bias_ready, 1)
                f(gate_r[:, :], ps[:, AUX, :], ACT.Sigmoid, bias=gate_bias[:, 0:1])
                f(gate_z, ps[:, AUX + 1, :], ACT.Sigmoid, bias=gate_bias[:, 1:2]).then_inc(rz_ready, 1)

            def candidate(b):
                act.wait_ge(t_ready, b + 1)
                f(hTs[:, :], cand, ACT.Tanh, bias=col(C_IN)).then_inc(n_ready, 1)

            def z_out(b):
                act.wait_ge(zT_full, b + 1)
                f(HT[:, b, :], ps[:, TB, :], ACT.Copy)
                f(hTs[:, :], ps[:, TB, :], ACT.Square).then_inc(z2_ready, 1)

            def scale_neighbours(b, k):
                hold(act, gathered[k], 16 * TOPK * (b + 1))
                for r in range(TOPK):
                    last = f(landing[:, k, r, :], landing[:, k, r, :], ACT.Copy,
                             scale=simil[:, bass.ds(TPB * b + k, 1), r])
                last.then_inc(scaled_ready, 1)

            def steps(p, b):
                h = NB * (p + 1) + b
                tail = (lambda: roots(h), lambda: rectify(h, b, p + 1), lambda: operand_out(h, b, p + 1))
                out_of = lambda: copy_out(p, b)
                return ((out_of, lambda: degree_roots(b), *tail),
                        (out_of, lambda: squares(1, b), lambda: norms(b), *tail),
                        (out_of, lambda: sigmoids(b), lambda: candidate(b), *tail),
                        (out_of, lambda: squares(3, b), lambda: z_out(b)),
                        (out_of, *(lambda k=k: scale_neighbours(b, k) for k in range(TPB))))[p]

            def over(at_units, p, b):
                return behind_units(at_units, steps(p, b))

            def upper_block(p, b, after):
                for u in range(UNITS):
                    if u in split_units(p, b):
                        act.wait_ge(at_loaded[u % SLOTS], loaded_value(NB * p + b, u))
                        if used_before(p, b, u) is not None:
                            act.wait_ge(used, used_before(p, b, u))
                        f(A_hi[:, staged_slot(p, b, u), :, :], ring[:, u % SLOTS, :, :],
                          ACT.Copy).then_inc(upper_ready, 1)
                    if u in after:
                        after[u]()

            def first_rectify(b):
                act.wait_ge(hT_full, b + 1)
                if b >= 2:
                    act.wait_ge(g_full, b - 1)
                f(HT[:, b, :], ps[:, first_hT[b % 2], :], ACT.Relu)
                f(first_hTs[b % 2][:, :], ps[:, first_hT[b % 2], :], ACT.Relu).then_inc(hTs_ready, 1)

            def first_operand_out(b):
                act.wait_ge(g_full, b + 1)
                f(flat(G_first, b), ps[:, first_G[b % 2], :], ACT.Copy).then_inc(g_ready, 1)

            act.wait_ge(consts_set, 1)
            f(spare[:, SPARES:SPARES + 1], ones[:, :], ACT.Sqrt)
            roots(0)
            for b in range(NB):
                if b + 1 < NB:
                    roots(b + 1, (b + 1) % 2)
                first_rectify(b)
                first_operand_out(b)
            act.wait_ge(g_ready, NB)
            for i, u in enumerate(SPLIT_FIRST):
                f(G_first_hi[:, i, :, :], G_first[:, u // 2, u % 2 * UK:u % 2 * UK + UK, :],
                  ACT.Copy).then_inc(firsthi_ready, 1)
            act.wait_ge(rest_loaded, 16)
            with act.Fori(1, NB) as b:
                upper_block(0, b, over(ACT_FIRST, 0, b - 1))
            for p in range(1, 4):
                upper_block(p, 0, over(ACT_TURN[p - 1], p - 1, NB - 1))
                with act.Fori(1, NB) as b:
                    upper_block(p, b, over(ACT_AT[p], p, b - 1))
            out_of, row_squares, z_copies = steps(3, NB - 1)
            out_of()
            z_copies()
            row_squares()

            def stage_tile(t, odd):
                if not (isinstance(t, int) and t <= 2):
                    act.wait_ge(half_full, 2 * t - 2)
                f((gate_r, hTs)[odd][:, 0:P], HT[:, :, :].rearrange("p b (t n) -> p (b t) n", n=P)[:, t, :],
                  ACT.Copy).then_inc(ztile_ready, 1)

            def pair_out(t, odd):
                if not (isinstance(t, int) and t < 2):
                    act.wait_ge(scanned, t - 1)
                for half in range(2):
                    hold(act, half_full, 2 * t + half + 1)
                    bank = pair_bank(4 * half)
                    f(scores[odd][:, half * (N // 2):(half + 1) * (N // 2)],
                      ps[:, bank:bank + 4, :].rearrange("p c n -> p (c n)"), ACT.Identity,
                      scale=2.0, bias=neg_sq[:, bass.ds(t, 1)]).then_inc(half_out, 1)

            def similarity(b):
                rows = simil[:, bass.ds(TPB * b, TPB), :]
                hold(act, clamp_ready, b + 1)
                f(rows, rows, ACT.Sqrt, scale=-1.0, bias=eps_d2[:, :]).then_inc(dist_ready, 1)
                hold(act, dist_ready, b + 1)
                f(rows, rows, ACT.Exp, scale=-0.5).then_inc(simil_ready, 1)

            def new_roots(b):
                rows = bass.ds(TPB * b, TPB)
                hold(act, deg2_ready, b + 1)
                f(root2[:, rows], deg2[:, rows], ACT.Sqrt).then_inc(root2_ready, 1)

            def scale_last(b):
                hold(act, d2_ready, b + 1)
                for n in range(TPB):
                    last = f(G_last[:, b, n, :], G_last[:, b, n, :], ACT.Copy,
                             scale=d2inv[:, bass.ds(TPB * b + n, 1)])
                last.then_inc(last_ready, 1)
                hold(act, last_ready, b + 1)
                f(flat(G_hi[1], b), flat(G_last, b), ACT.Copy).then_inc(lasthi_ready, 1)

            def tiles_out(b):
                behind = (similarity, new_roots, scale_last, None)
                for k in range(TPB):
                    t = TPB * b + k
                    pair_out(t, k % 2)
                    if not isinstance(t, int) or t + 2 < NT:
                        stage_tile(t + 2, k % 2)
                    if behind[k] and not (isinstance(b, int) and b == 0):
                        behind[k](b - 1)

            act.wait_ge(sqrow_full, NB)
            stage_tile(1, 1)
            act.wait_ge(negsq_ready, 1)
            act.wait_ge(zss_ready, NB)
            tiles_out(0)
            with act.Fori(1, NB - 1) as b:
                tiles_out(b)
            last = NB - 1
            pair_out(TPB * last, 0)
            stage_tile(TPB * last + 2, 0)
            similarity(last - 1)
            pair_out(TPB * last + 1, 1)
            stage_tile(TPB * last + 3, 1)
            new_roots(last - 1)
            pair_out(TPB * last + 2, 0)
            pair_out(TPB * last + 3, 1)
            scale_last(last - 1)
            upper_block(4, 0, {13: lambda: (similarity(last), new_roots(last), scale_last(last))})
            upper_block(4, 1, over(ACT_TURN[4], 4, 0))
            with act.Fori(2, NB) as b:
                upper_block(4, b, over(ACT_AT[4], 4, b - 1))
            for step in steps(4, NB - 1):
                step()

        @block.vector
        def _(dve):
            v = nc.vector
            own = Steps(dve, dve_step)

            def rows_of(t, b):
                return flat(t, b)

            def statistics(h, b, odd=0):
                for n in range(TPB):
                    last = v.bn_stats(stats[:, odd, n, :], X[:, b, n, :])
                own.add(last)
                hold(dve, dve_step, own.value())
                for n in range(TPB):
                    last = v.bn_aggr(meanvar[:, odd, n, :], stats[:, odd, n, :])
                last.then_inc(stats_ready, 1)

            def normalise(h, b, odd=0, rows=hn, ahead=1):
                dve.wait_ge(std_ready, h + 1)
                own.add(v.reciprocal(rstd[:, :], std[:, odd, :]))
                own.settle()
                if not isinstance(h, int) or h >= ahead:
                    dve.wait_ge(hT_full, h + 1 - ahead)
                for n in range(TPB):
                    last = v.tensor_scalar(rows[:, n, :], X[:, b, n, :], meanvar[:, odd, n, 0:1],
                                           rstd[:, n:n + 1], ALU.subtract, ALU.mult)
                last.then_inc(hn_ready, 1)

            def operand_rest(b, p):
                odd = p % 2
                dve.wait_ge(ghi_ready, NB * (p - 1) + b + 1)
                if p == 2:
                    last = v.tensor_tensor(flat(G_lo[odd], b), ps[:, GB, :], flat(G_hi[odd], b).bitcast(fp32),
                                           ALU.subtract)
                else:
                    for n in range(TPB):
                        last = v.scalar_tensor_tensor(
                            G_lo[odd][:, b, n, :], ps[:, GB, n * P:(n + 1) * P],
                            inv_root[:, b, 1 if p == 1 else 0, n:n + 1],
                            G_hi[odd][:, b, n, :].bitcast(fp32), ALU.mult, ALU.subtract)
                last.then_inc(g_ready, 1)

            def sum_pieces(b, after):
                if not (isinstance(b, int) and b == 0):
                    dve.wait_ge(colsum_ready, b)
                for u in range(UNITS):
                    dve.wait_ge(at_loaded[u % SLOTS], loaded_value(b, u))
                    half = colsum[:, u % 2 * UK:u % 2 * UK + UK, :]
                    if u < 2:
                        ins = v.tensor_copy(half, ring[:, u % SLOTS, :, :])
                    else:
                        dve.wait_ge(summed, UNITS * b + u - 1)
                        ins = v.tensor_tensor(half, half, ring[:, u % SLOTS, :, :], ALU.add)
                    ins.then_inc(summed, 1)
                    if u in split_units(0, b):
                        lower(0, b, u)
                    if u in after:
                        after[u]()
                dve.wait_ge(summed, UNITS * (b + 1))
                own.add(v.tensor_tensor(colsum[:, 0:2, :], colsum[:, 0:2, :], colsum[:, 2:4, :], ALU.add))
                own.settle()
                if isinstance(b, int) and b == 0:
                    dve.wait_ge(hT_full, NB)
                else:
                    dve.wait_ge(degree_full, b)
                v.tensor_tensor(folded, colsum[:, 0, :], colsum[:, 1, :], ALU.add).then_inc(colsum_ready, 1)

            def degrees(b):
                dve.wait_ge(degree_full, b + 1)
                if not (isinstance(b, int) and b == 0):
                    dve.wait_ge(root_ready, b)
                v.tensor_copy(degree[:, b, :], ps[:, AUX, 0:TPB])
                v.tensor_copy(deg_pair[:, 0, :], ps[:, AUX, 0:TPB])
                v.tensor_scalar(deg_pair[:, 1, :], ps[:, AUX, 0:TPB], 1.0, None, ALU.add).then_inc(pair_ready, 1)

            def inverse_roots(b):
                dve.wait_ge(root_ready, b + 1)
                v.reciprocal(inv_root[:, b, :, :], deg_root[:, :, :]).then_inc(inv_ready, 1)

            def add_rows(p, b):
                dve.wait_ge(nat_full, NB * p + b + 1)
                own.add(v.tensor_tensor(rows_of(X, b), rows_of(X, b), ps[:, TB, :], ALU.add))
                hold(dve, dve_step, own.value())

            def l1_rows(b):
                q = NB + b
                dve.wait_ge(nat_full, q + 1)
                sums = nat[:, :, :].rearrange("p t f -> p (t f)")
                own.add(v.tensor_tensor(sums, rows_of(G_lo[1], b).bitcast(fp32), ps[:, TB, :], ALU.add))
                own.settle()
                own.add(v.tensor_tensor(sums, sums, rows_of(G_hi[1], b).bitcast(fp32), ALU.add))
                own.settle()
                for n in range(TPB):
                    last = v.scalar_tensor_tensor(nat[:, n, :], nat[:, n, :], inv_root[:, b, 1, n:n + 1],
                                                  w(ROW_L1), ALU.mult, ALU.add)
                last.then_inc(v_ready, 1)

            def square_floor(b):
                dve.wait_ge(ss_ready, b + 1)
                v.tensor_scalar(ssum[:, :], ssum[:, :], 1e-24, None, ALU.max).then_inc(ssmax_ready, 1)

            def add_unit_rows(b):
                dve.wait_ge(norm_ready, b + 1)
                own.add(v.reciprocal(rstd[:, :], norm[:, :]))
                own.settle()
                for n in range(TPB):
                    last = v.scalar_tensor_tensor(X[:, b, n, :], nat[:, n, :], rstd[:, n:n + 1], X[:, b, n, :],
                                                  ALU.mult, ALU.add)
                own.add(last)
                hold(dve, dve_step, own.value())

            def reset(b):
                dve.wait_ge(rz_ready, b + 1)
                own.add(v.scalar_tensor_tensor(cand, ps[:, AUX + 3, :], col(C_HN), gate_r[:, :],
                                               ALU.add, ALU.mult))
                own.settle()
                v.tensor_tensor(cand, cand, ps[:, AUX + 2, :], ALU.add).then_inc(t_ready, 1)

            def update(b):
                dve.wait_ge(n_ready, b + 1)
                own.add(v.tensor_tensor(cand, HT[:, b, :], hTs[:, :], ALU.subtract))
                own.settle()
                own.add(v.tensor_tensor(cand, cand, gate_z, ALU.mult))
                own.settle()
                v.tensor_tensor(cand, cand, hTs[:, :], ALU.add).then_inc(u_ready, 1)

            def lap_rows(b):
                dve.wait_ge(nat_full, 3 * NB + b + 1)
                for n in range(TPB):
                    last = v.scalar_tensor_tensor(nat[:, n, :], ps[:, TB, n * P:(n + 1) * P],
                                                  inv_root[:, b, 0, n:n + 1], w(ROW_LAP1), ALU.mult, ALU.add)
                own.add(last)
                own.settle()
                z = nat[:, :, :].rearrange("p t f -> p (t f)")
                v.scalar_tensor_tensor(z, z, 0.1, z, ALU.mult, ALU.max).then_inc(z_ready, 1)

            def square_parts(b):
                dve.wait_ge(sqrow_full, b + 1)
                row = ps[0:3, GB, :]
                own.add(v.tensor_copy(part_hi[:, :], row))
                own.settle()
                own.add(v.tensor_tensor(rest[:, :], row, part_hi[:, :], ALU.subtract))
                own.settle()
                own.add(v.tensor_copy(part_mid[:, :], rest[:, :]))
                own.settle()
                own.add(v.tensor_tensor(rest[:, :], rest[:, :], part_mid[:, :], ALU.subtract))
                own.add(v.tensor_scalar(mixed[:, :], part_hi[:, :], pack[0:3, 0:1], None, ALU.mult))
                own.settle()
                own.add(v.scalar_tensor_tensor(mixed[:, :], part_mid[:, :], pack[0:3, 1:2], mixed[:, :],
                                               ALU.mult, ALU.add))
                own.settle()
                v.scalar_tensor_tensor(sq_aug[:, b, :], rest[:, :], pack[0:3, 2:3], mixed[:, :],
                                       ALU.mult, ALU.add).then_inc(aug_ready, 1)
                sums = neg_sq[:, bass.ds(TPB * b, TPB)]
                hold(dve, zss_ready, b + 1)
                v.tensor_scalar(sums, sums, -1.0, None, ALU.mult).then_inc(negsq_ready, 1)

            def steps(p, b):
                h = NB * (p + 1) + b
                tail = (lambda: normalise(h, b), lambda: operand_rest(b, p + 1))
                return ((lambda: degrees(b), lambda: (inverse_roots(b), add_rows(0, b), statistics(h, b)), *tail),
                        (lambda: l1_rows(b), lambda: square_floor(b),
                         lambda: (add_unit_rows(b), statistics(h, b)), *tail),
                        (lambda: reset(b), lambda: update(b),
                         lambda: (add_rows(2, b), statistics(h, b)), *tail),
                        (lambda: lap_rows(b), lambda: square_parts(b)),
                        (lambda: weigh(b, 0), lambda: weigh(b, 1), lambda: weigh(b, 2), lambda: weigh(b, 3),
                         lambda: last_rows(b)))[p]

            def over(at_units, p, b):
                return behind_units(at_units, steps(p, b))

            def lower(p, b, u):
                slot = staged_slot(p, b, u)
                dve.wait_ge(upper_ready, split_count(p, b, u))
                v.tensor_tensor(A_lo[:, slot, :, :], ring[:, u % SLOTS, :, :],
                                A_hi[:, slot, :, :].bitcast(fp32), ALU.subtract).then_inc(lower_ready, 1)

            def lower_block(p, b, after):
                for u in range(UNITS):
                    if u in split_units(p, b):
                        lower(p, b, u)
                    if u in after:
                        after[u]()

            def whole_rows(p, j):
                u = WHOLE[p][j]
                m, kk = u // 2, u % 2 * UK
                dve.wait_ge(used, UNITS * NB * p)
                dve.wait_ge(g_ready, NB * p + m + 1)
                v.tensor_tensor(G_whole[:, j, :, :], G_hi[p % 2][:, m, kk:kk + UK, :].bitcast(fp32),
                                G_lo[p % 2][:, m, kk:kk + UK, :].bitcast(fp32), ALU.add).then_inc(whole_ready, 1)

            def with_whole_rows(p, after):
                both = dict(after)
                for j, u in enumerate(WHOLE_AT[p]):
                    first = after.get(u, lambda: None)
                    both[u] = lambda j=j, first=first: (first(), whole_rows(p, j))
                return both

            def counted(loop, bodies, expected, first=1):
                start = own.value()
                with loop as b:
                    own.turn(start + (b - first) * expected)
                    bodies(b)
                    assert own.n == expected, own.n
                return start

            def first_rows(b):
                if b + 1 < NB:
                    dve.wait_ge(x_loaded[b + 1], 16)
                    statistics(b + 1, b + 1, (b + 1) % 2)
                normalise(b, b, b % 2, first_hn[b % 2], 2)

            dve.wait_ge(x_loaded[0], 16)
            statistics(0, 0)
            normalise(0, 0, 0, first_hn[0], 2)
            dve.wait_ge(x_loaded[1], 16)
            statistics(1, 1, 1)
            first_rows(1)

            sum_pieces(0, {2 * b - 4: lambda b=b: first_rows(b) for b in range(2, NB)})
            for i, u in enumerate(SPLIT_FIRST):
                dve.wait_ge(firsthi_ready, i + 1)
                v.tensor_tensor(G_first_lo[:, i, :, :], G_first[:, u // 2, u % 2 * UK:u % 2 * UK + UK, :],
                                G_first_hi[:, i, :, :].bitcast(fp32), ALU.subtract).then_inc(firstlo_ready, 1)
            dve.wait_ge(rest_loaded, 16)
            v.tensor_tensor(gate_bias[:, :], pack[:, 16 * P + C_IR:16 * P + C_IR + 2],
                            pack[:, 16 * P + C_HR:16 * P + C_HR + 2], ALU.add).then_inc(bias_ready, 1)
            start = counted(dve.Fori(1, NB), lambda b: sum_pieces(b, over(DVE_FIRST, 0, b - 1)), DVE_STEPS[0])
            own.turn(start + (NB - 1) * DVE_STEPS[0])
            for p in range(1, 4):
                lower_block(p, 0, with_whole_rows(p, over(DVE_TURN[p - 1], p - 1, NB - 1)))
                start = counted(dve.Fori(1, NB),
                                lambda b: lower_block(p, b, over(DVE_AT[p], p, b - 1)), DVE_STEPS[p])
                own.turn(start + (NB - 1) * DVE_STEPS[p])
            for step in steps(3, NB - 1):
                step()

            def scan(t):
                dve.wait_ge(half_out, 2 * t + 2)
                row = scores[t % 2][:, :]
                own.add(v.max(best[:, t, :], row))
                own.settle()
                v.max_index(best_at[:, t, :], best[:, t, :], row).then_inc(scanned, 1)

            def clamp(b):
                own.settle()
                v.tensor_scalar(simil[:, TPB * b:TPB * (b + 1), :], best[:, TPB * b:TPB * (b + 1), 0:TOPK],
                                0.0, None, ALU.min).then_inc(clamp_ready, 1)

            def new_degrees(b):
                rows = slice(TPB * b, TPB * (b + 1))
                dve.wait_ge(simil_ready, b + 1)
                own.add(v.reduce_sum(deg2[:, rows], simil[:, rows, :], axis=mybir.AxisListType.X))
                own.settle()
                v.tensor_tensor(deg2[:, rows], deg2[:, rows], degree[:, b, :], ALU.add).then_inc(deg2_ready, 1)

            def new_inverse(b):
                rows = slice(TPB * b, TPB * (b + 1))
                dve.wait_ge(root2_ready, b + 1)
                v.reciprocal(d2inv[:, rows], root2[:, rows]).then_inc(d2_ready, 1)

            def last_rest(b):
                dve.wait_ge(lasthi_ready, b + 1)
                v.tensor_tensor(flat(G_lo[1], b), flat(G_last, b), flat(G_hi[1], b).bitcast(fp32),
                                ALU.subtract).then_inc(lastlo_ready, 1)

            behind = (new_degrees, new_inverse, last_rest)
            for t in range(NT - 2):
                scan(t)
                if t % TPB == TPB - 1:
                    clamp(t // TPB)
                elif t >= TPB:
                    behind[t % TPB](t // TPB - 1)

            def weigh(b, k):
                dve.wait_ge(scaled_ready, TPB * b + k + 1)
                slot = landing[:, k, :, :]
                own.add(v.tensor_tensor(slot[:, 0:2, :], slot[:, 0:2, :], slot[:, 2:4, :], ALU.add))
                own.settle()
                v.tensor_tensor(near[:, k, :], slot[:, 0, :], slot[:, 1, :], ALU.add).then_inc(weighted, 1)

            def last_rows(b):
                dve.wait_ge(weighted, TPB * b + TPB)
                dve.wait_ge(nat_full, 4 * NB + b + 1)
                own.add(v.tensor_tensor(nat[:, :, :].rearrange("p t f -> p (t f)"), near[:, :, :].rearrange("p t f -> p (t f)"),
                                        ps[:, TB, :], ALU.add))
                own.settle()
                for n in range(TPB):
                    last = v.scalar_tensor_tensor(nat[:, n, :], nat[:, n, :],
                                                  d2inv[:, bass.ds(b * TPB + n, 1)],
                                                  w(ROW_LAP2), ALU.mult, ALU.add)
                own.add(last)
                own.settle()
                v.tensor_tensor(rows_of(X, b), rows_of(X, b), nat[:, :, :].rearrange("p t f -> p (t f)"),
                                ALU.add).then_inc(x_final, 1)

            lower_block(4, 0, {0: lambda: (scan(NT - 2), last_rest(NB - 2)),
                               9: lambda: (scan(NT - 1), clamp(NB - 1)),
                               11: lambda: new_degrees(NB - 1), 13: lambda: new_inverse(NB - 1),
                               14: lambda: last_rest(NB - 1)})
            lower_block(4, 1, over(DVE_TURN[4], 4, 0))
            start = counted(dve.Fori(2, NB),
                            lambda b: lower_block(4, b, over(DVE_AT[4], 4, b - 1)), DVE_STEPS[4], 2)
            own.turn(start + (NB - 2) * DVE_STEPS[4])
            for step in steps(4, NB - 1):
                step()

        @block.gpsimd
        def _(pool):
            g = nc.gpsimd
            g.memset(ones3[:, :], 1.0)
            g.memset(halves[:, :], -0.5)
            g.memset(ones[:, :], 1.0)
            g.memset(eps_ln[:, :], 1e-5)
            g.memset(eps_d2[:, :], 1e-10).then_inc(consts_set, 1)

            for b in range(NB):
                pool.wait_ge(last_ready, b + 1)
                pool.dma_start(scaled_rows.rearrange("(b t p) f -> b p t f", t=TPB, p=P)[b],
                               G_last[:, b, :, :]).then_inc(rows_stored, 16)
            pool.wait_ge(rows_stored, 16 * NB)
            pool.wait_ge(scanned, NT)

            def gather(t, k):
                if not (isinstance(t, int) and t < GSLOTS):
                    pool.wait_ge(weighted, t - GSLOTS + 1)
                g.tensor_copy(picks[:, k, :], best_at[:, t, 0:TOPK]).then_inc(picks_ready, 1)
                hold(pool, picks_ready, t + 1)
                for r in range(TOPK):
                    pool.indirect_dma_start(
                        out=landing[:, k, r, :], out_offset=None, in_=scaled_rows,
                        in_offset=bass.IndirectOffsetOnAxis(ap=picks[:, k, r:r + 1], axis=0),
                    ).then_inc(gathered[k], 16)

            for k in range(GSLOTS):
                gather(k, k)
            with pool.Fori(1, NT // GSLOTS) as turn:
                for k in range(GSLOTS):
                    gather(GSLOTS * turn + k, k)


PE_FIRST, ACT_FIRST, DVE_FIRST = (0, 7, 10), (0, 1, 7, 10, 13), (5, 7, 9, 15)
PE_AT = {1: (0, 10, 11), 2: (0, 6, 10, 11), 3: (0, 6, 9), 4: (2,)}
ACT_AT = {1: (4, 7, 8, 10, 13, 15), 2: (0, 5, 6, 11, 13, 14), 3: (2, 6, 10), 4: (2, 3, 7, 8, 11)}
DVE_AT = {1: (4, 6, 8, 11, 15), 2: (5, 7, 9, 11, 14), 3: (3, 14), 4: (3, 6, 8, 11, 14)}
PE_TURN = {0: (0, 9, 10), 1: (0, 10, 11), 2: (0, 5, 10, 11), 4: (3,)}
ACT_TURN = {0: (1, 7, 10, 12, 13), 1: (4, 7, 8, 11, 13, 15), 2: (0, 5, 6, 11, 13, 14), 4: (2, 9, 12, 15, 15)}
DVE_TURN = {0: (3, 6, 9, 13), 1: (4, 5, 8, 11, 15), 2: (5, 6, 8, 11, 14), 4: (10, 13, 15, 15, 15)}
WHOLE_AT = {1: (2, 3, 10, 15), 2: (2, 4, 11, 15), 3: (1, 4, 11, 15)}
DVE_STEPS = (4, 6, 6, 7, 6)


def kernel(**inputs):
    import numpy as np
    import concourse.bacc as bacc
    from concourse.bass_utils import run_bass_kernel_spmd

    fp32 = mybir.dt.float32
    get = lambda n: np.asarray(inputs[n])
    x = np.ascontiguousarray(get("x").reshape(NB, TPB, P, P).transpose(2, 0, 1, 3))
    at = np.ascontiguousarray(get("adj").reshape(NB, BLK, UNITS, UK, P).transpose(0, 2, 4, 3, 1))
    w0, w1, wm = get("L0_gnn_W"), get("L1_gnn_W"), get("L2_gnn_W_msg")
    wi, wh = get("L2_gnn_W_ih"), get("L2_gnn_W_hh")
    bi, bh = get("L2_gnn_b_ih").reshape(3, P), get("L2_gnn_b_hh").reshape(3, P)
    mats = [np.eye(P, dtype=np.float32), w0[:, :P].T, w0[:, P:].T, w1.T, wm.T]
    mats += [wi[g * P:(g + 1) * P].T for g in range(3)] + [wh[g * P:(g + 1) * P].T for g in range(3)]
    mats += [get("L3_gnn_W1"), get("L3_gnn_W2")]
    mats += [np.broadcast_to(get(n), (P, P)) for n in ("L1_gnn_b", "L3_gnn_b1", "L3_gnn_b2")]
    cols = [get("L0_gnn_b"), get("L2_gnn_b_msg"), bi[0], bi[1], bi[2], bh[0], bh[1], bh[2]]
    pack = np.ascontiguousarray(np.concatenate(mats + [c.reshape(P, 1) for c in cols], axis=1))

    nc = bacc.Bacc("TRN2", target_bir_lowering=False, num_devices=1, dynamic_dma_scratch_size=8192)
    arrays = {"x_rows": x, "adj_t": at, "packed": pack}
    aps = [nc.dram_tensor(n, a.shape, fp32, kind="ExternalInput").ap() for n, a in arrays.items()]
    scaled_rows = nc.dram_tensor("scaled_rows", (N, P), fp32, kind="Internal").ap()
    out = nc.dram_tensor("out_rows", (NB, P, TPB, P), fp32, kind="ExternalOutput").ap()
    gnn_stack(nc, *aps, scaled_rows, out)
    r = run_bass_kernel_spmd(nc, [arrays], core_ids=[0])
    got = r.results[0]["out_rows"]
    return np.ascontiguousarray(got.transpose(0, 2, 1, 3)).reshape(N, P)
```
